# Optimizing a Trainium2 kernel written in Bass

```python
import numpy as np
import jax
import jax.numpy as jnp

def _softmax(x, axis=-1):
    return jax.nn.softmax(x, axis=axis)

def _gelu(x):
    return jax.nn.gelu(x, approximate=True)

def _silu(x):
    return jax.nn.silu(x)

def _sigmoid(x):
    return jax.nn.sigmoid(x)

def _layernorm(x, axis=-1, eps=1e-05):
    m = jnp.mean(x, axis=axis, keepdims=True)
    v = jnp.var(x, axis=axis, keepdims=True)
    return (x - m) / jnp.sqrt(v + eps)

def _scatter_add(tgt, idx, src, axis=0):
    return tgt.at[idx].add(src)

def _segment_sum(src, seg, n):
    return jax.ops.segment_sum(src, seg, n)
kernel_name = 'mk_seq_postln_d1_jaxref_r4_cc93b3'

def setup_inputs(seed: int=0):
    np.random.seed(seed)
    _w = jnp.asarray

    def _L0_attn_setup():
        import jax, jax.numpy as jnp
        import numpy as np
        FILTER_ORDER = 64

        def _pos_embedding(seq_len, dim):
            position = jnp.arange(seq_len, dtype=jnp.float32)[:, None]
            div_term = jnp.exp(jnp.arange(0, dim, 2, dtype=jnp.float32) * (-jnp.log(10000.0) / dim))
            ang = position * div_term
            pe = jnp.zeros((seq_len, dim), dtype=jnp.float32)
            pe = pe.at[:, 0::2].set(jnp.sin(ang))
            pe = pe.at[:, 1::2].set(jnp.cos(ang))
            return pe
        key = jax.random.key(seed)
        k1, k2, k3 = jax.random.split(key, 3)
        B, L, D = (4, 1024, 256)
        x = jax.random.normal(k1, (B, L, D), dtype=jnp.float32)
        W1 = jax.random.normal(k2, (FILTER_ORDER, D), dtype=jnp.float32) * (1.0 / np.sqrt(FILTER_ORDER))
        b1 = jnp.zeros((D,), dtype=jnp.float32)
        W2 = jax.random.normal(k3, (D, D), dtype=jnp.float32) * (1.0 / np.sqrt(D))
        b2 = jnp.zeros((D,), dtype=jnp.float32)
        return {'x': x, 'W1': W1, 'b1': b1, 'W2': W2, 'b2': b2}
    _L0_attn_in = _L0_attn_setup()

    def _L0_ffn_setup():
        import jax, jax.numpy as jnp
        import numpy as np
        NUM_EXPERTS = 8
        TOP_K = 2
        CAPACITY_FACTOR = 1.25
        key = jax.random.key(seed)
        ks = jax.random.split(key, 5)
        B, S, D, H, E = (4, 512, 256, 512, NUM_EXPERTS)
        scale = 0.02
        return {'x': jax.random.normal(ks[0], (B, S, D), dtype=jnp.float32), 'gate_w': jax.random.normal(ks[1], (E, D), dtype=jnp.float32) * scale, 'gate_proj_w': jax.random.normal(ks[2], (E, H, D), dtype=jnp.float32) * scale, 'up_proj_w': jax.random.normal(ks[3], (E, H, D), dtype=jnp.float32) * scale, 'down_proj_w': jax.random.normal(ks[4], (E, D, H), dtype=jnp.float32) * scale}
    _L0_ffn_in = _L0_ffn_setup()
    _d = {'L0_attn_x': _L0_attn_in['x'], 'L0_attn_W1': _L0_attn_in['W1'], 'L0_attn_b1': _L0_attn_in['b1'], 'L0_attn_W2': _L0_attn_in['W2'], 'L0_attn_b2': _L0_attn_in['b2'], 'L0_ffn_gate_w': _L0_ffn_in['gate_w'], 'L0_ffn_gate_proj_w': _L0_ffn_in['gate_proj_w'], 'L0_ffn_up_proj_w': _L0_ffn_in['up_proj_w'], 'L0_ffn_down_proj_w': _L0_ffn_in['down_proj_w']}
    _x0 = _d['L0_attn_x']
    _d['L0_attn_x'] = jax.random.normal(jax.random.fold_in(jax.random.key(seed), 1), (2, 2048, 256), dtype=_x0.dtype)
    del _x0
    return _d

def reference(L0_attn_x, L0_attn_W1, L0_attn_b1, L0_attn_W2, L0_attn_b2, L0_ffn_gate_w, L0_ffn_gate_proj_w, L0_ffn_up_proj_w, L0_ffn_down_proj_w):

    def _L0_attn_ref(x, W1, b1, W2, b2):
        import jax, jax.numpy as jnp
        import numpy as np
        FILTER_ORDER = 64

        def _pos_embedding(seq_len, dim):
            position = jnp.arange(seq_len, dtype=jnp.float32)[:, None]
            div_term = jnp.exp(jnp.arange(0, dim, 2, dtype=jnp.float32) * (-jnp.log(10000.0) / dim))
            ang = position * div_term
            pe = jnp.zeros((seq_len, dim), dtype=jnp.float32)
            pe = pe.at[:, 0::2].set(jnp.sin(ang))
            pe = pe.at[:, 1::2].set(jnp.cos(ang))
            return pe
        B, L, D = x.shape
        pos_emb = _pos_embedding(L, FILTER_ORDER)
        h = jax.nn.gelu(pos_emb @ W1 + b1, approximate=False)
        filt = h @ W2 + b2
        n = 2 * L
        x_fft = jnp.fft.rfft(x, n=n, axis=1)
        f_fft = jnp.fft.rfft(filt[None, :, :], n=n, axis=1)
        out = jnp.fft.irfft(x_fft * f_fft, n=n, axis=1)[:, :L, :]
        return out

    def _L0_ffn_ref(x, gate_w, gate_proj_w, up_proj_w, down_proj_w):
        import jax, jax.numpy as jnp
        import numpy as np
        NUM_EXPERTS = 8
        TOP_K = 2
        CAPACITY_FACTOR = 1.25
        B, S, D = x.shape
        E, K = (NUM_EXPERTS, TOP_K)
        T = B * S
        xf = x.reshape(T, D)
        logits = xf @ gate_w.T
        probs = jax.nn.softmax(logits, axis=-1)
        top_p, top_i = jax.lax.top_k(probs, K)
        w = top_p / (jnp.sum(top_p, axis=-1, keepdims=True) + 1e-09)
        capacity = int(CAPACITY_FACTOR * T / E)
        oh = jax.nn.one_hot(top_i, E, dtype=jnp.int32)
        rank = jnp.cumsum(oh, axis=0) - 1
        my_rank = jnp.sum(rank * oh, axis=-1)
        keep = (my_rank < capacity).astype(w.dtype)
        comb = jnp.einsum('tk,tke->te', w * keep, oh.astype(w.dtype))
        out = jnp.zeros_like(xf)
        for e in range(E):
            g = jax.nn.silu(xf @ gate_proj_w[e].T)
            u = xf @ up_proj_w[e].T
            y = g * u @ down_proj_w[e].T
            out = out + comb[:, e:e + 1] * y
        return out.reshape(B, S, D)
    x = L0_attn_x
    x = _layernorm(x + _L0_attn_ref(x, L0_attn_W1, L0_attn_b1, L0_attn_W2, L0_attn_b2), axis=-1)
    x = _layernorm(x + _L0_ffn_ref(x, L0_ffn_gate_w, L0_ffn_gate_proj_w, L0_ffn_up_proj_w, L0_ffn_down_proj_w), axis=-1)
    return x

_drawn_inputs = setup_inputs


def setup_inputs(seed=0):
    import zlib

    import numpy as np

    out = dict(_drawn_inputs(seed))
    spreads = {'L0_attn_b1': (0.0, 0.1), 'L0_attn_b2': (0.0, 0.1)}
    factors = {'L0_ffn_gate_w': 4.017,
     'L0_ffn_gate_proj_w': 3.601,
     'L0_ffn_up_proj_w': 3.581,
     'L0_ffn_down_proj_w': 3.575}
    for name, (base, spread) in spreads.items():
        noise = np.random.default_rng([zlib.crc32(name.encode()), seed]).standard_normal(out[name].shape)
        drawn = base * np.exp(spread * noise) if base else spread * noise
        out[name] = jnp.asarray(drawn.astype(out[name].dtype))
    for name, factor in factors.items():
        out[name] = (out[name] * factor).astype(out[name].dtype)
    return out
```

```python
from contextlib import ExitStack

import numpy as np

import concourse.bass as bass
from concourse import mybir

P = 128
B, L, D = 2, 2048, 256
T = B * L
NI = T // P
FO = 64
N1, N2 = L // P, P
DH = D // 2
GD = P // N1
GROUPS = DH // GD
SEQ = B + 1
COLS = SEQ * DH
ADD_CH = 16
E, H, K = 8, 512, 2
CAP = int(1.25 * T / E)
RT = CAP // P
HALF = CAP // 2
ROWS = E * CAP
ZR = 4
DC, HC = D // P, H // P
WPART = DC * H
WSCALE = 16.0
EPS = 1e-5
OUT_OF_RANGE = 32768.0

F32 = mybir.dt.float32
F16 = mybir.dt.float16
U32 = mybir.dt.uint32
ALU = mybir.AluOpType
ACT = mybir.ActivationFunctionType
X = mybir.AxisListType.X


def constants():
    f = np.float32
    c = {}
    pos = np.arange(L, dtype=f)[:, None]
    div = np.exp(np.arange(0, FO, 2, dtype=f) * f(-np.log(f(10000.0)) / f(FO)))
    ang = (pos * div).astype(f)
    pe = np.zeros((L, FO), f)
    pe[:, 0::2] = np.sin(ang)
    pe[:, 1::2] = np.cos(ang)
    c["posT"] = np.ascontiguousarray(pe.T)
    n1 = np.arange(N1)[:, None]
    k1 = np.arange(N1)[None, :]
    th = 2 * np.pi * n1 * (k1 + 0.25) / N1
    across = np.zeros((GD, N1, N1, 2, GD))
    for d in range(GD):
        across[d, :, :, 0, d] = np.cos(th)
        across[d, :, :, 1, d] = -np.sin(th)
    c["across"] = across.reshape(P, 2 * N1 * GD).astype(f)
    n2 = np.arange(N2, dtype=np.float64)
    within = np.zeros((N1, P, 6, P))
    for k in range(N1):
        ph = 2 * np.pi * np.outer(n2, k + 0.25 + N1 * n2) / L
        within[k, :, 0] = np.cos(ph)
        within[k, :, 1] = -np.sin(ph)
        within[k, :, 2] = np.sin(ph)
        within[k, :, 3] = np.cos(ph).T / L
        within[k, :, 4] = np.sin(ph).T / L
        within[k, :, 5] = -np.sin(ph).T / L
    c["within"] = within.reshape(N1, P, 6 * P).astype(f)
    back = np.zeros((4, N1, 2, B, B, N1, 4))
    for q in range(4):
        for b in range(B):
            back[q, :, 0, b, b, :, q] = np.cos(th).T
            back[q, :, 1, b, b, :, q] = -np.sin(th).T
    c["back"] = back.reshape(P, B * P).astype(f)
    c["ident"] = np.eye(P, dtype=f)
    c["below"] = np.triu(np.ones((P, P)), 1).astype(f)
    rows = np.zeros((P, 2 * NI * K * E // 2 + K * E + E), f)
    mask = np.ones((K * E, NI))
    mask[:, 0] = 0
    rows[:, 0:512] = mask.reshape(-1)
    rows[:, 512:528] = np.tile(np.arange(E) * CAP, K)
    rows[:, 528:536] = E - np.arange(E)
    c["rows"] = rows
    return c


def build(nc, xT, xN, W1, b1, W2, b2, gateT, experts, posT, across, within, back, ident, below, rows, out):
    fil_dram = nc.dram_tensor("fil_dram", (D, L), F32, kind="Internal").ap()
    xg_dram = [nc.dram_tensor(f"xg{k}_dram", (ROWS, D), F32, kind="Internal").ap() for k in range(K)]
    y_dram = [nc.dram_tensor(f"y{k}_dram", (ROWS, D), F32, kind="Internal").ap() for k in range(K)]

    ctx = ExitStack()
    with ctx:
        def sem(name):
            return ctx.enter_context(nc.semaphore(name))

        def sb(stack, name, shape, dt=F32):
            return stack.enter_context(nc.sbuf_tensor(name, shape, dt))

        xn = sb(ctx, "xn", [P, NI, D])
        c_ident = sb(ctx, "c_ident", [P, P])
        c_below = sb(ctx, "c_below", [P, P])
        c_rows = sb(ctx, "c_rows", [P, 536])
        c_gate = sb(ctx, "c_gate", [P, DC, E])
        stats = sb(ctx, "stats", [P, NI, 6])
        lnt = sb(ctx, "lnt", [P, 6, NI])
        w_top = sb(ctx, "w_top", [P, K, NI])
        idx_put = sb(ctx, "idx_put", [P, K, NI], U32)
        idx_get = sb(ctx, "idx_get", [P, K, NI], U32)

        conv = ExitStack()
        c_across = sb(conv, "c_across", [P, 2 * N1 * GD])
        c_back = sb(conv, "c_back", [P, B, P])
        ring = [sb(conv, f"ring{s}", [P, 8, N2]) for s in range(2)]
        x1 = sb(conv, "x1", [P, 2 * N1, COLS])
        mats = [sb(conv, f"mats{s}", [P, 6, P]) for s in range(4)]
        fhat = [sb(conv, f"fhat{s}", [P, 3, DH]) for s in range(2)]
        prod = [sb(conv, f"prod{s}", [P, 2, 2, B, DH]) for s in range(2)]
        yhat = [sb(conv, f"yhat{s}", [P, 2, B * DH]) for s in range(2)]
        z = sb(conv, "z", [P, B * DH * 2 * N1])
        zt = [sb(conv, f"zt{s}", [P, B, ADD_CH * 32]) for s in range(2)]
        w1 = sb(conv, "w1", [FO, D])
        w2 = sb(conv, "w2", [P, DC, D])
        bias = sb(conv, "bias", [P, 2, DC])
        pos = sb(conv, "pos", [FO, L])
        hT = sb(conv, "hT", [P, DC, L])
        fT = z.rearrange("p (c l) -> p c l", c=4)[:, 0:DC, :]
        zeros = sb(conv, "zeros", [P, ZR * D])[:, :]
        conv.close()

        moe = ExitStack()
        wh = sb(moe, "wh", [P, E, 3 * WPART], F16)
        wl = sb(moe, "wl", [P, E, 3 * WPART], F16)
        wst = [sb(moe, f"wst{s}", [P, WPART]) for s in range(2)]
        xg = [sb(moe, f"xg{s}", [P, RT, D]) for s in range(2)]
        xth = sb(moe, "xth", [P, DC, CAP], F16)
        xtl = sb(moe, "xtl", [P, DC, CAP], F16)
        ah = [sb(moe, f"ah{s}", [P, HC, CAP], F16) for s in range(2)]
        al = [sb(moe, f"al{s}", [P, HC, CAP], F16) for s in range(2)]
        s32 = [sb(moe, f"s32_{s}", [P, HALF]) for s in range(2)]
        a32 = [sb(moe, f"a32_{s}", [P, HALF]) for s in range(2)]
        ysb = [sb(moe, f"ysb{s}", [P, RT, D]) for s in range(2)]
        yg = [sb(moe, f"yg{s}", [P, D]) for s in range(4)]
        fin = [sb(moe, f"fin{s}", [P, D]) for s in range(4)]
        moe.close()

        gate = ExitStack()
        xst = [sb(gate, f"xst{s}", [P, D]) for s in range(4)]
        xts = [sb(gate, f"xts{s}", [P, DC, P]) for s in range(4)]
        rt = sb(gate, "rt", [P, 10, NI * E])
        small = sb(gate, "small", [P, 12, NI])
        oh = sb(gate, "oh", [P, K, E, NI])
        scan = sb(gate, "scan", [P, K, E, NI])
        rk = sb(gate, "rk", [P, K, E, NI])
        rk2 = sb(gate, "rk2", [P, K, E, NI])
        red = sb(gate, "red", [P, 6, K, NI])
        tot = sb(gate, "tot", [P, K * E])
        base = sb(gate, "base", [P, K * E])
        gate.close()

        ps = ctx.enter_context(nc.psum_tensor("ps", [P, 8, 512], F32))

        in_filter, in_across, in_back, in_xn, in_const = (sem(n) for n in ("in_filter", "in_across", "in_back", "in_xn", "in_const"))
        in_ring = [sem(f"in_ring{s}") for s in range(2)]
        in_mats = [sem(f"in_mats{s}") for s in range(4)]
        fil_stored, zero_stored = sem("fil_stored"), sem("zero_stored")
        put_done = [sem(f"put_done{k}") for k in range(K)]
        in_xg = [sem(f"in_xg{s}") for s in range(2)]
        in_w = [sem(f"in_w{s}") for s in range(2)]
        y_stored = [sem(f"y_stored{s}") for s in range(2)]
        in_yg = [sem(f"in_yg{s}") for s in range(4)]
        out_stored = sem("out_stored")
        h_full, h_done, f_full, f_done, zeros_set = (sem(n) for n in ("h_full", "h_done", "f_full", "f_done", "zeros_set"))
        x1_full, x1_done = sem("x1_full"), sem("x1_done")
        fwd_full, fhat_done, prod_done, y_ready = (sem(n) for n in ("fwd_full", "fhat_done", "prod_done", "y_ready"))
        z_full, z_done = sem("z_full"), sem("z_done")
        zt_done, back_full, added = sem("zt_done"), sem("back_full"), sem("added")
        st_done, ln_step, sq_done = sem("st_done"), sem("ln_step"), sem("sq_done")
        xst_done, xst_kept, xst_turned, xts_done, logits_full = (sem(n) for n in ("xst_done", "xst_kept", "xst_turned", "xts_done", "logits_full"))
        r_step, e_ready, e_done, tot_ready, base_full, idx_ready = (sem(n) for n in ("r_step", "e_ready", "e_done", "tot_ready", "base_full", "idx_ready"))
        xt_full, xth_done, xtl_done = sem("xt_full"), sem("xth_done"), sem("xtl_done")
        wh_done, wl_done = sem("wh_done"), sem("wl_done")
        gu_full, s_done, a_done, ah_done, al_done = (sem(n) for n in ("gu_full", "s_done", "a_done", "ah_done", "al_done"))
        y_full, y_done = sem("y_full"), sem("y_done")
        yg_used = sem("yg_used")
        fin_step, fin_var, fin_sq, fin_done = sem("fin_step"), sem("fin_var"), sem("fin_sq"), sem("fin_done")

        XT_PER = (RT + 1) // 2
        Q_PER = 2 * HC
        src_x = xT.rearrange("b (h s g p) (n m) -> b h s (p n) g m", h=2, s=2, g=8, n=N1)
        src_f = fil_dram.rearrange("(h s g p) (n m) -> h s (p n) g m", h=2, s=2, g=8, n=N1)
        xg_v = [t.rearrange("(n j p) d -> n p j d", j=RT, p=P) for t in xg_dram]
        y_v = [t.rearrange("(n j p) d -> n p j d", j=RT, p=P) for t in y_dram]
        xg_zero = [t.rearrange("(p n r) d -> n p (r d)", p=P, r=ZR) for t in xg_dram]
        xn_in = xN.rearrange("(p i) d -> p (i d)", p=P)
        out_v = out.rearrange("(p i) d -> p i d", p=P)

        block = ctx.enter_context(nc.Block())

        @block.sync
        def _(sp):
            for dst, src in ((w1[:, :], W1), (bias[:, 0, :], b1), (pos[:, :], posT), (w2[:, :, :], W2), (bias[:, 1, :], b2)):
                sp.dma_start(dst, src).then_inc(in_filter, 16)
            sp.dma_start(c_across[:, :], across).then_inc(in_across, 16)

            def load_ring(s, m, src):
                sp.wait_ge(x1_full, 8 * m + 4 * s + 4)
                sp.dma_start(ring[s][:, :, :], src).then_inc(in_ring[s], 16)

            def load_mats(s, n, k):
                sp.wait_ge(z_done, n + 1)
                sp.dma_start(mats[s][:, :, :], within[k].rearrange("p (m c) -> p m c", m=6)).then_inc(in_mats[s], 16)

            with sp.Fori(0, 2) as h:
                with sp.Fori(0, B) as b:
                    for s in range(2):
                        load_ring(s, h * SEQ + b, src_x[b, h, s])
                sp.wait_ge(fil_stored, 32)
                for s in range(2):
                    load_ring(s, h * SEQ + B, src_f[h, s])
                with sp.Fori(0, N1 // 4) as k4:
                    k = 4 * k4
                    for s in range(4):
                        load_mats(s, h * N1 + k + s, k + s)

            def load_rows(s, k, e):
                n = k * E + e
                sp.wait_ge(xt_full, XT_PER * (n + 1))
                sp.dma_start(xg[s][:, :, :], xg_v[k][e]).then_inc(in_xg[s], 16)

            def load_weights(e, parity):
                for j in range(3):
                    s = (3 * parity + j) % 2
                    sp.wait_ge(wl_done, 3 * e + j + 1)
                    sp.dma_start(wst[s][:, :], experts[e, :, j * WPART:(j + 1) * WPART]).then_inc(in_w[s], 16)

            def store_y(s, k, e):
                n = k * E + e
                sp.wait_ge(y_done, 2 + RT * (n + 1))
                sp.dma_start(y_v[k][e], ysb[s][:, :, :]).then_inc(y_stored[s], 16)

            sp.wait_ge(idx_ready, 1)
            load_weights(0, 0)
            sp.wait_ge(put_done[0], 16 * NI)
            load_rows(0, 0, 0)
            with sp.Fori(0, (E - 2) // 2) as e2:
                e = 2 * e2
                for s in range(2):
                    load_rows(1 - s, 0, e + s + 1)
                    load_weights(e + s + 1, 1 - s)
                    store_y(s, 0, e + s)
            load_rows(1, 0, E - 1)
            load_weights(E - 1, 1)
            store_y(0, 0, E - 2)
            sp.wait_ge(put_done[1], 16 * NI)
            load_rows(0, 1, 0)
            store_y(1, 0, E - 1)
            with sp.Fori(0, (E - 2) // 2) as e2:
                e = 2 * e2
                for s in range(2):
                    load_rows(1 - s, 1, e + s + 1)
                    store_y(s, 1, e + s)
            load_rows(1, 1, E - 1)
            store_y(0, 1, E - 2)
            store_y(1, 1, E - 1)
            with sp.Fori(0, NI // 4) as g:
                sp.wait_ge(fin_done, 4 + 4 * (g + 1))
                sp.dma_start(out_v[:, bass.ds(4 * g, 4), :], xn[:, bass.ds(4 * g, 4), :]).then_inc(out_stored, 16)
            sp.wait_ge(out_stored, 16 * (NI // 4))

        @block.gpsimd
        def _(pool):
            nc.gpsimd.memset(zeros, 0.0).then_inc(zeros_set, 1)
            pool.wait_ge(zeros_set, 1)
            for k in range(K):
                with pool.Fori(0, ROWS // P // ZR) as n:
                    pool.dma_start(xg_zero[k][n], zeros).then_inc(zero_stored, 16)
            pool.sem_inc(xst_kept, 4)
            with pool.Fori(0, NI // 4) as i4:
                i = 4 * i4
                for s in range(4):
                    pool.wait_ge(xst_done, i + s + 1)
                    nc.gpsimd.tensor_copy(xn[:, bass.ds(i + s, 1), :], xst[s][:, :].unsqueeze(1)).then_inc(xst_kept, 1)
            pool.wait_ge(xst_kept, 4 + NI)
            pool.wait_ge(zero_stored, 16 * K * (ROWS // P // ZR))
            pool.wait_ge(idx_ready, 1)
            for k in range(K):
                for i in range(NI):
                    nc.gpsimd.indirect_dma_start(
                        xg_dram[k][:, :], bass.IndirectOffsetOnAxis(ap=idx_put[:, k, i:i + 1], axis=0), xn[:, i, :], None,
                        bounds_check=ROWS - 1, oob_is_err=False).then_inc(put_done[k], 16)
            pool.sem_inc(yg_used, 4)
            for k in range(K):
                for s in range(2):
                    pool.wait_ge(y_stored[s], 16 * (E // 2) * (k + 1))
                for i in range(NI):
                    pool.wait_ge(yg_used, k * NI + i + 1)
                    nc.gpsimd.indirect_dma_start(
                        yg[i % 4][:, :], None, y_dram[k][:, :],
                        bass.IndirectOffsetOnAxis(ap=idx_get[:, k, i:i + 1], axis=0)).then_inc(in_yg[i % 4], 16)

        @block.scalar
        def _(act):
            act.sem_inc(x1_done, 4)
            act.sem_inc(z_done, 4)
            act.sem_inc(y_done, 2)
            act.wait_ge(in_filter, 80)
            for n in range(DC * 4):
                act.wait_ge(h_full, n + 1)
                nc.scalar.activation(hT[:, n // 4, (n % 4) * 512:(n % 4 + 1) * 512], ps[:, n % 4, :], ACT.Gelu,
                                     bias=bias[:, 0, n // 4:n // 4 + 1]).then_inc(h_done, 1)
            for n in range(DC * 4):
                act.wait_ge(f_full, n + 1)
                nc.scalar.activation(fT[:, n // 4, (n % 4) * 512:(n % 4 + 1) * 512], ps[:, 4 + n % 4, :], ACT.Identity,
                                     bias=bias[:, 1, n // 4:n // 4 + 1]).then_inc(f_done, 1)
                if n % 4 == 3:
                    act.wait_ge(f_done, n + 1)
                    act.dma_start(fil_dram[(n // 4) * P:(n // 4 + 1) * P, :], fT[:, n // 4, :]).then_inc(fil_stored, 16)

            act.dma_start(xn[:, :, :].rearrange("p i d -> p (i d)"), xn_in).then_inc(in_xn, 16)
            act.dma_start(c_back[:, :, :], back.rearrange("p (b m) -> p b m", b=B)).then_inc(in_back, 16)
            for dst, src in ((c_ident[:, :], ident), (c_below[:, :], below), (c_rows[:, :], rows), (c_gate[:, :, :], gateT)):
                act.dma_start(dst, src).then_inc(in_const, 16)

            def keep_x1(u, bank, col):
                act.wait_ge(x1_full, 8 + u + 1)
                nc.scalar.activation(
                    x1[:, :, bass.ds(col, 2 * GD)].rearrange("p k (g d) -> p k g d", g=2),
                    ps[:, bank, :].rearrange("p (g k d) -> p k g d", g=2, d=GD), ACT.Copy).then_inc(x1_done, 1)

            def keep_fhat(n, s):
                act.wait_ge(fwd_full, n + 1)
                act.wait_ge(prod_done, 2 * n + 2)
                nc.scalar.activation(fhat[s][:, 0:2, :], ps[:, 2 * s:2 * s + 2, B * DH:COLS], ACT.Copy).then_inc(fhat_done, 1)
                nc.scalar.activation(fhat[s][:, 2, :], ps[:, 2 * s, B * DH:COLS], ACT.Copy).then_inc(fhat_done, 1)

            zv = z.rearrange("p (c k) -> p k c", k=2 * N1)

            def keep_z(n, k, s):
                act.wait_ge(z_full, n + 1)
                nc.scalar.activation(zv[:, bass.ds(2 * k, 2), :], ps[:, 4 + s, :].rearrange("p (r c) -> p r c", r=2),
                                     ACT.Copy).then_inc(z_done, 1)

            with act.Fori(0, 2) as h:
                with act.Fori(0, SEQ) as q:
                    for j in range(GROUPS // 2):
                        keep_x1((h * SEQ + q) * (GROUPS // 2) + j, j % 4, q * DH + j * 2 * GD)
                keep_fhat(h * N1, 0)
                with act.Fori(0, (N1 - 2) // 2) as k2:
                    k = 2 * k2
                    for s in range(2):
                        keep_fhat(h * N1 + k + s + 1, 1 - s)
                        keep_z(h * N1 + k + s, k + s, s)
                keep_fhat(h * N1 + N1 - 1, 1)
                keep_z(h * N1 + N1 - 2, N1 - 2, 0)
                keep_z(h * N1 + N1 - 1, N1 - 1, 1)

            act.wait_ge(ln_step, 6)
            nc.scalar.activation(lnt[:, 5, :], lnt[:, 3, :], ACT.Sqrt).then_inc(sq_done, 1)
            with act.Fori(0, NI // 4) as i4:
                i = 4 * i4
                for s in range(4):
                    act.wait_ge(xst_turned, 4 + i + s + 1)
                    nc.scalar.activation(xts[s][:, :, :], ps[:, s, 0:D].rearrange("p (c t) -> p c t", c=DC),
                                         ACT.Copy).then_inc(xts_done, 1)
            act.wait_ge(e_ready, 1)
            nc.scalar.activation(rt[:, 2, :], rt[:, 1, :], ACT.Exp).then_inc(e_done, 1)

            def turn_hi(n, j):
                w = 2 if 2 * j + 1 < RT else 1
                act.wait_ge(xt_full, 2 * XT_PER + XT_PER * n + j + 1)
                nc.scalar.activation(
                    xth[:, :, 2 * j * P:(2 * j + w) * P].rearrange("p c (t r) -> p t c r", t=w),
                    ps[:, 4 + j % 2, 0:w * D].rearrange("p (t c r) -> p t c r", t=w, c=DC), ACT.Copy).then_inc(xth_done, 1)

            def weights_hi(e, parity):
                for j in range(3):
                    s = (3 * parity + j) % 2
                    act.wait_ge(in_w[s], 24 * (e - parity) + 16 * ((3 * parity + j) // 2 + 1))
                    nc.scalar.activation(wh[:, bass.ds(e, 1), j * WPART:(j + 1) * WPART],
                                         wst[s][:, :].unsqueeze(1), ACT.Copy, scale=WSCALE).then_inc(wh_done, 1)

            def a_hi(n, s, j):
                act.wait_ge(a_done, 2 + Q_PER * n + j + 1)
                nc.scalar.activation(ah[s][:, j // 2, (j % 2) * HALF:(j % 2 + 1) * HALF], a32[j % 2][:, :],
                                     ACT.Copy).then_inc(ah_done, 1)

            def expert(n, s, split, turn, first=False):
                for j in range(Q_PER):
                    act.wait_ge(gu_full, Q_PER * n + j + 1)
                    act.wait_ge(a_done, Q_PER * n + j + 1)
                    nc.scalar.activation(s32[j % 2][:, :], ps[:, 2 * (j % 2), 0:HALF], ACT.Silu, scale=1.0 / WSCALE).then_inc(s_done, 1)
                    if j:
                        a_hi(n, s, j - 1)
                a_hi(n, s, Q_PER - 1)
                if turn:
                    for j in range(XT_PER):
                        turn_hi(n + 1, j)
                if split:
                    weights_hi(n + 1, 1 - s)
                if not first:
                    act.wait_ge(y_stored[s], 8 * (n - s))
                for j in range(RT):
                    act.wait_ge(y_full, RT * n + j + 1)
                    nc.scalar.activation(ysb[s][:, j, :], ps[:, 6 + (RT * s + j) % 2, 0:D], ACT.Copy,
                                         scale=1.0 / WSCALE).then_inc(y_done, 1)

            weights_hi(0, 0)
            for j in range(XT_PER):
                turn_hi(0, j)
            for e in range(2):
                expert(e, e, True, True, first=True)
            with act.Fori(1, (E - 2) // 2) as e2:
                e = 2 * e2
                for s in range(2):
                    expert(e + s, s, True, True)
            expert(E - 2, 0, True, True)
            expert(E - 1, 1, False, True)
            with act.Fori(E // 2, (2 * E - 2) // 2) as n2:
                n = 2 * n2
                for s in range(2):
                    expert(n + s, s, False, True)
            expert(2 * E - 2, 0, False, True)
            expert(2 * E - 1, 1, False, False)
            with act.Fori(0, NI // 4) as g:
                act.wait_ge(fin_var, g + 1)
                nc.scalar.activation(lnt[:, 5, 0:4], lnt[:, 3, 0:4], ACT.Sqrt).then_inc(fin_sq, 1)

        @block.tensor
        def _(pe):
            pe.sem_inc(x1_full, 8)
            pe.sem_inc(xst_turned, 4)
            pe.sem_inc(xt_full, 2 * XT_PER)
            mm = nc.tensor.matmul
            pe.wait_ge(in_filter, 80)
            for n in range(DC * 4):
                if n >= 4:
                    pe.wait_ge(h_done, n - 3)
                mm(ps[:, n % 4, :], w1[:, (n // 4) * P:(n // 4 + 1) * P], pos[:, (n % 4) * 512:(n % 4 + 1) * 512],
                   start=True, stop=True).then_inc(h_full, 1)
            for n in range(DC * 4):
                pe.wait_ge(h_done, DC * 4)
                if n >= 4:
                    pe.wait_ge(f_done, n - 3)
                for c in range(DC):
                    last = mm(ps[:, 4 + n % 4, :], w2[:, c, (n // 4) * P:(n // 4 + 1) * P],
                              hT[:, c, (n % 4) * 512:(n % 4 + 1) * 512], start=(c == 0), stop=(c == DC - 1))
                last.then_inc(f_full, 1)

            def go_across(m):
                for s in range(2):
                    pe.wait_ge(in_ring[s], 16 * (m + 1))
                    for j in range(4):
                        u = m * 8 + s * 4 + j
                        pe.wait_ge(x1_done, u + 1)
                        for g in range(2):
                            last = mm(ps[:, j, g * 256:(g + 1) * 256], ring[s][:, 2 * j + g, :], c_across[:, :],
                                      start=True, stop=True)
                        last.then_inc(x1_full, 1)

            def forward(n, k, s, ms):
                pe.wait_ge(in_mats[ms], 4 * (n - ms) + 16)
                pe.wait_ge(prod_done, 2 * n + 2)
                re = x1[:, bass.ds(2 * k, 1), :].rearrange("p a c -> p (a c)")
                im = x1[:, bass.ds(2 * k + 1, 1), :].rearrange("p a c -> p (a c)")
                m = mats[ms]
                mm(ps[:, 2 * s, 0:COLS], m[:, 0, :], re, start=True, stop=False)
                mm(ps[:, 2 * s, 0:COLS], m[:, 2, :], im, start=False, stop=True)
                mm(ps[:, 2 * s + 1, 0:COLS], m[:, 1, :], re, start=True, stop=False)
                mm(ps[:, 2 * s + 1, 0:COLS], m[:, 0, :], im, start=False, stop=True).then_inc(fwd_full, 1)

            def inverse(n, s, ms):
                pe.wait_ge(y_ready, 4 + 2 * n + 2)
                pe.wait_ge(z_done, n + 3)
                m = mats[ms]
                mm(ps[:, 4 + s, 0:256], m[:, 3, :], yhat[s][:, 0, :], start=True, stop=False)
                mm(ps[:, 4 + s, 0:256], m[:, 5, :], yhat[s][:, 1, :], start=False, stop=True)
                mm(ps[:, 4 + s, 256:512], m[:, 4, :], yhat[s][:, 0, :], start=True, stop=False)
                mm(ps[:, 4 + s, 256:512], m[:, 3, :], yhat[s][:, 1, :], start=False, stop=True).then_inc(z_full, 1)

            pe.wait_ge(in_across, 16)
            with pe.Fori(0, 2) as h:
                with pe.Fori(0, SEQ) as q:
                    go_across(h * SEQ + q)
                pe.wait_ge(x1_done, 4 + 24 * (h + 1))
                forward(h * N1, 0, 0, 0)
                with pe.Fori(0, (N1 - 4) // 4) as k4:
                    k = 4 * k4
                    for j in range(4):
                        forward(h * N1 + k + j + 1, k + j + 1, (j + 1) % 2, (j + 1) % 4)
                        inverse(h * N1 + k + j, j % 2, j)
                for k in range(N1 - 4, N1):
                    if k + 1 < N1:
                        forward(h * N1 + k + 1, k + 1, (k + 1) % 2, (k + 1) % 4)
                    inverse(h * N1 + k, k % 2, k % 4)
                pe.wait_ge(in_back, 16)
                with pe.Fori(0, DH // ADD_CH // 2) as c2:
                    c = 2 * c2
                    for s in range(2):
                        pe.wait_ge(zt_done, 2 * (h * (DH // ADD_CH) + c + s + 1))
                        for b in range(B):
                            last = mm(ps[:, 6 + s, :], c_back[:, b, :], zt[s][:, b, :], start=(b == 0), stop=(b == B - 1))
                        last.then_inc(back_full, 1)

            pe.wait_ge(in_const, 64)
            with pe.Fori(0, NI // 4) as i4:
                i = 4 * i4
                for s in range(4):
                    pe.wait_ge(xst_done, i + s + 1)
                    for c in range(DC):
                        last = nc.tensor.transpose(ps[:, s, c * P:(c + 1) * P], xst[s][:, c * P:(c + 1) * P], c_ident[:, :])
                    last.then_inc(xst_turned, 1)
                for s in range(4):
                    pe.wait_ge(xts_done, i + s + 1)
                    for c in range(DC):
                        last = mm(ps[:, 4, bass.ds((i + s) * E, E)], xts[s][:, c, :], c_gate[:, c, :],
                                  start=(c == 0), stop=(c == DC - 1), skip_group_check=True)
                    last.then_inc(logits_full, 1)
            pe.wait_ge(tot_ready, 1)
            mm(ps[:, 5, 0:K * E], c_below[:, :], tot[:, :], start=True, stop=True).then_inc(base_full, 1)

            def turn(n, s):
                pe.wait_ge(in_xg[s], 8 * (n - s) + 16)
                for j in range(XT_PER):
                    if j == 2:
                        pe.wait_ge(xtl_done, XT_PER * n + 1)
                    for t in range(2 * j, min(2 * j + 2, RT)):
                        for c in range(DC):
                            o = (t % 2) * D + c * P
                            last = nc.tensor.transpose(ps[:, 4 + j % 2, o:o + P], xg[s][:, t, c * P:(c + 1) * P], c_ident[:, :])
                    last.then_inc(xt_full, 1)

            def split_mm(o, whi, wlo, xhi, xlo, start, stop):
                mm(o, whi, xhi, start=start, stop=False)
                mm(o, whi, xlo, start=False, stop=False)
                return mm(o, wlo, xhi, start=False, stop=stop)

            def wslice(w, e, off, width):
                return w[:, bass.ds(e, 1), off:off + width].rearrange("p a c -> p (a c)")

            def expert(n, e, s, split, turn_next):
                pe.wait_ge(xtl_done, XT_PER * (n + 1))
                if split:
                    pe.wait_ge(wl_done, 2 + 3 * (e + 1))
                for j in range(Q_PER):
                    pe.wait_ge(a_done, Q_PER * n + j + 1)
                    r = slice((j % 2) * HALF, (j % 2 + 1) * HALF)
                    for part in range(2):
                        for c in range(DC):
                            off = part * WPART + c * H + (j // 2) * P
                            last = split_mm(ps[:, 2 * (j % 2) + part, 0:HALF], wslice(wh, e, off, P), wslice(wl, e, off, P),
                                            xth[:, c, r], xtl[:, c, r], c == 0, c == DC - 1)
                    last.then_inc(gu_full, 1)
                if turn_next:
                    turn(n + 1, 1 - s)
                pe.wait_ge(al_done, 2 + Q_PER * (n + 1))
                for t in range(RT):
                    pe.wait_ge(y_done, RT * n + t + 1)
                    for c in range(HC):
                        off = 2 * WPART + c * D
                        last = split_mm(ps[:, 6 + (RT * s + t) % 2, 0:D], ah[s][:, c, t * P:(t + 1) * P], al[s][:, c, t * P:(t + 1) * P],
                                        wslice(wh, e, off, D), wslice(wl, e, off, D), c == 0, c == HC - 1)
                    last.then_inc(y_full, 1)

            turn(0, 0)
            with pe.Fori(0, (E - 2) // 2) as e2:
                e = 2 * e2
                for s in range(2):
                    expert(e + s, e + s, s, True, True)
            expert(E - 2, E - 2, 0, True, True)
            expert(E - 1, E - 1, 1, True, True)
            with pe.Fori(0, (E - 2) // 2) as e2:
                e = 2 * e2
                for s in range(2):
                    expert(E + e + s, e + s, s, False, True)
            expert(2 * E - 2, E - 2, 0, False, True)
            expert(2 * E - 1, E - 1, 1, False, False)

        @block.vector
        def _(dve):
            v = nc.vector
            dve.sem_inc(prod_done, 4)
            dve.sem_inc(wl_done, 2)
            dve.sem_inc(a_done, 2)
            dve.sem_inc(fin_done, 4)
            dve.sem_inc(y_ready, 4)
            dve.sem_inc(al_done, 2)

            def multiply(n, s):
                dve.wait_ge(fhat_done, 2 * n + 2)
                xs = ps[:, 2 * s:2 * s + 2, 0:B * DH].rearrange("p r (b d) -> p r b d", b=B)
                dve.wait_ge(y_ready, 2 * n + 2)
                for w in range(2):
                    v.tensor_tensor(prod[s][:, w], xs, fhat[s][:, w:w + 2, :].unsqueeze(2).to_broadcast([P, 2, B, DH]),
                                    ALU.mult).then_inc(prod_done, 1)
                dve.wait_ge(prod_done, 2 * n + 6)
                dve.wait_ge(z_done, n + 3)
                for w, op in ((0, ALU.subtract), (1, ALU.add)):
                    v.tensor_tensor(yhat[s][:, w, :].rearrange("p (b d) -> p b d", b=B), prod[s][:, w, 0], prod[s][:, w, 1], op).then_inc(y_ready, 1)

            with dve.Fori(0, 2) as h:
                with dve.Fori(0, N1 // 2) as k2:
                    k = 2 * k2
                    for s in range(2):
                        multiply(h * N1 + k + s, s)
                dve.wait_ge(z_done, 4 + N1 * (h + 1))
                for c in range(0, DH // ADD_CH, 2):
                    for s in range(2):
                        for b in range(B):
                            off = (c + s) * (ADD_CH * 32) + b * DH * 32
                            v.transpose(zt[s][:, b, :], z[:, off:off + ADD_CH * 32]).then_inc(zt_done, 1)
                    dve.wait_ge(in_xn, 16)
                    for s in range(2):
                        dve.wait_ge(back_full, h * (DH // ADD_CH) + c + s + 1)
                        dst = xn[:, :, bass.ds(h * DH + (c + s) * ADD_CH, ADD_CH)].rearrange("p i d -> p d i")
                        v.tensor_tensor(dst, ps[:, 6 + s, :].rearrange("p (d i) -> p d i", i=NI), dst, ALU.add).then_inc(added, 1)

            def norm_steps(st, cols, step, count):
                steps = [
                    lambda: v.tensor_tensor(lnt[:, 0, 0:cols], st[:, :, 1], st[:, :, 4], ALU.add),
                    lambda: v.tensor_tensor(lnt[:, 1, 0:cols], st[:, :, 1], st[:, :, 4], ALU.subtract),
                    lambda: v.tensor_tensor(lnt[:, 2, 0:cols], st[:, :, 2], st[:, :, 5], ALU.add),
                    lambda: v.tensor_tensor(lnt[:, 1, 0:cols], lnt[:, 1, 0:cols], lnt[:, 1, 0:cols], ALU.mult),
                    lambda: v.scalar_tensor_tensor(lnt[:, 3, 0:cols], lnt[:, 1, 0:cols], D / 4.0, lnt[:, 2, 0:cols], ALU.mult, ALU.add),
                    lambda: v.tensor_scalar(lnt[:, 3, 0:cols], lnt[:, 3, 0:cols], 1.0 / D, EPS, ALU.mult, ALU.add),
                    lambda: v.tensor_scalar(lnt[:, 4, 0:cols], lnt[:, 0, 0:cols], 0.5, None, ALU.mult),
                ]
                return steps

            dve.wait_ge(added, 2 * DH // ADD_CH)
            with dve.Fori(0, NI) as i:
                v.bn_stats(stats[:, bass.ds(i, 1), :].rearrange("p a c -> p (a c)"),
                           xn[:, bass.ds(i, 1), :].rearrange("p a c -> p (a c)")).then_inc(st_done, 1)
            dve.wait_ge(st_done, NI)
            for n, step in enumerate(norm_steps(stats, NI, ln_step, 0)):
                dve.wait_ge(ln_step, n)
                step().then_inc(ln_step, 1)
            dve.wait_ge(sq_done, 1)
            v.reciprocal(lnt[:, 5, :], lnt[:, 5, :]).then_inc(ln_step, 1)
            dve.wait_ge(ln_step, 8)
            with dve.Fori(0, NI // 4) as i4:
                i = 4 * i4
                for s in range(4):
                    dve.wait_ge(xst_turned, i + s + 1)
                    dve.wait_ge(xst_kept, i + s + 1)
                    v.tensor_scalar(xst[s][:, :], xn[:, bass.ds(i + s, 1), :].rearrange("p a c -> p (a c)"),
                                    lnt[:, 4, bass.ds(i + s, 1)], lnt[:, 5, bass.ds(i + s, 1)],
                                    ALU.subtract, ALU.mult).then_inc(xst_done, 1)

            count = [0]

            def step(ins):
                ins.then_inc(r_step, 1)
                count[0] += 1
                dve.wait_ge(r_step, count[0])

            def ie(k):
                return rt[:, k, :].rearrange("p (i e) -> p i e", e=E)

            def over_e(ap):
                return ap.unsqueeze(2).to_broadcast([P, NI, E])

            first_of = c_rows[:, 528:536].unsqueeze(1).to_broadcast([P, NI, E])
            region = c_rows[:, 512:528].rearrange("p (k e) -> p k e", k=K).unsqueeze(3).to_broadcast([P, K, E, NI])
            dve.wait_ge(logits_full, NI)
            step(v.tensor_copy(rt[:, 0, :], ps[:, 4, 0:NI * E]))
            step(v.tensor_reduce(small[:, 0, :], ie(0), X, ALU.max))
            v.tensor_tensor(ie(1), ie(0), over_e(small[:, 0, :]), ALU.subtract).then_inc(e_ready, 1)
            dve.wait_ge(e_done, 1)
            step(v.tensor_reduce(small[:, 1, :], ie(2), X, ALU.add))
            step(v.reciprocal(small[:, 2, :], small[:, 1, :]))
            step(v.tensor_tensor(ie(3), ie(2), over_e(small[:, 2, :]), ALU.mult))
            for k in range(K):
                p_k, top = ie(3 + k), small[:, 3 + k, :]
                hot = oh[:, k].rearrange("p e i -> p i e")
                step(v.tensor_reduce(top, p_k, X, ALU.max))
                step(v.tensor_tensor(ie(5), p_k, over_e(top), ALU.is_equal))
                step(v.tensor_tensor(ie(6), ie(5), first_of, ALU.mult))
                step(v.tensor_reduce(small[:, 5, :], ie(6), X, ALU.max))
                step(v.tensor_tensor(ie(7), first_of, over_e(small[:, 5, :]), ALU.is_equal))
                step(v.tensor_copy(hot, ie(7)))
                if k == 0:
                    step(v.scalar_tensor_tensor(rt[:, 4, :], rt[:, 7, :], -2.0, rt[:, 3, :], ALU.mult, ALU.add))
            step(v.tensor_tensor(small[:, 6, :], small[:, 3, :], small[:, 4, :], ALU.add))
            step(v.tensor_scalar(small[:, 6, :], small[:, 6, :], 1e-9, None, ALU.add))
            step(v.reciprocal(small[:, 7, :], small[:, 6, :]))
            flat = lambda t: t.rearrange("p k e i -> p (k e i)")
            step(v.tensor_tensor_scan(flat(scan), c_rows[:, 0:512], flat(oh), 0.0, ALU.mult, ALU.add))
            v.tensor_copy(tot[:, :], scan[:, :, :, NI - 1].rearrange("p k e -> p (k e)")).then_inc(tot_ready, 1)
            dve.wait_ge(base_full, 1)
            step(v.tensor_copy(base[:, :], ps[:, 5, 0:K * E]))
            step(v.tensor_tensor(rk[:, :], scan[:, :],
                                 base[:, :].rearrange("p (k e) -> p k e", k=K).unsqueeze(3).to_broadcast([P, K, E, NI]), ALU.add))
            step(v.tensor_tensor(rk2[:, :], rk[:, :], oh[:, :], ALU.mult))
            step(v.tensor_reduce(red[:, 0], rk2[:, :].rearrange("p k e i -> p k i e"), X, ALU.add))
            step(v.tensor_tensor(rk[:, :], region, oh[:, :], ALU.mult))
            step(v.tensor_reduce(red[:, 1], rk[:, :].rearrange("p k e i -> p k i e"), X, ALU.add))
            step(v.tensor_scalar(red[:, 2], red[:, 0], float(CAP), None, ALU.is_le))
            step(v.scalar_tensor_tensor(red[:, 3], red[:, 0], -1.0, red[:, 1], ALU.add, ALU.add))
            step(v.tensor_tensor(red[:, 4], red[:, 3], red[:, 2], ALU.mult))
            step(v.tensor_scalar(red[:, 5], red[:, 2], -OUT_OF_RANGE, OUT_OF_RANGE, ALU.mult, ALU.add))
            step(v.tensor_tensor(red[:, 5], red[:, 5], red[:, 4], ALU.add))
            step(v.tensor_copy(idx_get[:, :, :], red[:, 4]))
            step(v.tensor_tensor(w_top[:, :, :], small[:, 3:5, :], small[:, 7, :].unsqueeze(1).to_broadcast([P, K, NI]), ALU.mult))
            step(v.tensor_tensor(w_top[:, :, :], w_top[:, :, :], red[:, 2], ALU.mult))
            dve.wait_ge(xst_kept, 4 + NI)
            dve.wait_ge(zero_stored, 16 * K * (ROWS // P // ZR))
            v.tensor_copy(idx_put[:, :, :], red[:, 5]).then_inc(idx_ready, 1)

            def turn_lo(n, j):
                w = 2 if 2 * j + 1 < RT else 1
                dve.wait_ge(xth_done, XT_PER * n + j + 1)
                cols = lambda t: t[:, :, 2 * j * P:(2 * j + w) * P].rearrange("p c (t r) -> p t c r", t=w)
                v.tensor_tensor(cols(xtl), ps[:, 4 + j % 2, 0:w * D].rearrange("p (t c r) -> p t c r", t=w, c=DC),
                                cols(xth), ALU.subtract).then_inc(xtl_done, 1)

            def weights_lo(e, parity):
                for j in range(3):
                    s = (3 * parity + j) % 2
                    dve.wait_ge(wh_done, 3 * e + j + 1)
                    part = lambda t: t[:, bass.ds(e, 1), j * WPART:(j + 1) * WPART].rearrange("p a c -> p (a c)")
                    v.scalar_tensor_tensor(part(wl), wst[s][:, :], WSCALE, part(wh), ALU.mult, ALU.subtract).then_inc(wl_done, 1)

            def a_lo(n, s, j):
                dve.wait_ge(ah_done, Q_PER * n + j + 1)
                r = slice((j % 2) * HALF, (j % 2 + 1) * HALF)
                v.tensor_tensor(al[s][:, j // 2, r], a32[j % 2][:, :], ah[s][:, j // 2, r], ALU.subtract).then_inc(al_done, 1)

            def expert(n, s, split, turn, add=None):
                for j in range(Q_PER):
                    dve.wait_ge(s_done, Q_PER * n + j + 1)
                    dve.wait_ge(al_done, Q_PER * n + j + 1)
                    v.scalar_tensor_tensor(a32[j % 2][:, :], ps[:, 2 * (j % 2) + 1, 0:HALF], 1.0 / WSCALE, s32[j % 2][:, :],
                                           ALU.mult, ALU.mult).then_inc(a_done, 1)
                    if j:
                        a_lo(n, s, j - 1)
                a_lo(n, s, Q_PER - 1)
                if turn:
                    for j in range(XT_PER):
                        turn_lo(n + 1, j)
                if split:
                    weights_lo(n + 1, 1 - s)
                if add is not None:
                    for j in range(4):
                        add_choice(0, 4 * add + j, add, j)

            def add_choice(k, i, turn4, j, to=None):
                dve.wait_ge(in_yg[j], 16 * (k * (NI // 4) + turn4 + 1))
                col = xn[:, bass.ds(i, 1), :].rearrange("p a c -> p (a c)")
                v.scalar_tensor_tensor(col if to is None else to, yg[j][:, :], w_top[:, k, bass.ds(i, 1)], col, ALU.mult, ALU.add).then_inc(yg_used, 1)

            weights_lo(0, 0)
            for j in range(XT_PER):
                turn_lo(0, j)
            with dve.Fori(0, (E - 2) // 2) as e2:
                e = 2 * e2
                for s in range(2):
                    expert(e + s, s, True, True)
            expert(E - 2, 0, True, True)
            expert(E - 1, 1, False, True)
            with dve.Fori(0, (E - 2) // 2) as e2:
                e = 2 * e2
                for s in range(2):
                    expert(E + e + s, s, False, True, add=e + s)
            expert(2 * E - 2, 0, False, True, add=E - 2)
            expert(2 * E - 1, 1, False, False, add=E - 1)
            with dve.Fori(0, NI // 4) as g:
                dve.wait_ge(fin_done, 4 * g + 4)
                for j in range(4):
                    add_choice(1, 4 * g + j, g, j, to=fin[j][:, :])
                dve.wait_ge(yg_used, 4 + NI + 4 * g + 4)
                for j in range(4):
                    v.bn_stats(stats[:, j, :], fin[j][:, :]).then_inc(fin_step, 1)
                dve.wait_ge(fin_step, g * 12 + 4)
                for n, st in enumerate(norm_steps(stats[:, 0:4, :], 4, None, 0)):
                    ins = st()
                    if n == 5:
                        ins.then_inc(fin_var, 1)
                        dve.wait_ge(fin_var, g + 1)
                    else:
                        ins.then_inc(fin_step, 1)
                        dve.wait_ge(fin_step, g * 12 + 4 + (n + 1 if n < 5 else n))
                dve.wait_ge(fin_sq, g + 1)
                v.reciprocal(lnt[:, 4 + 1, 4:8], lnt[:, 5, 0:4]).then_inc(fin_step, 2)
                dve.wait_ge(fin_step, g * 12 + 12)
                for j in range(4):
                    col = xn[:, bass.ds(4 * g + j, 1), :].rearrange("p a c -> p (a c)")
                    v.tensor_scalar(col, fin[j][:, :], lnt[:, 4, j:j + 1], lnt[:, 5, 4 + j:5 + j], ALU.subtract, ALU.mult).then_inc(fin_done, 1)


def kernel(L0_attn_x, L0_attn_W1, L0_attn_b1, L0_attn_W2, L0_attn_b2, L0_ffn_gate_w, L0_ffn_gate_proj_w,
           L0_ffn_up_proj_w, L0_ffn_down_proj_w):
    import concourse.bacc as bacc
    from concourse.bass_utils import run_bass_kernel_spmd

    x = np.asarray(L0_attn_x)
    turned = [np.asarray(w).reshape(E, H, DC, P).transpose(0, 3, 2, 1).reshape(E, P, DC * H)
              for w in (L0_ffn_gate_proj_w, L0_ffn_up_proj_w)]
    down = np.asarray(L0_ffn_down_proj_w).reshape(E, D, HC, P).transpose(0, 3, 2, 1).reshape(E, P, HC * D)
    arrays = {
        "xT": x.transpose(0, 2, 1),
        "xN": x.reshape(T, D),
        "W1": np.asarray(L0_attn_W1),
        "b1": np.asarray(L0_attn_b1).reshape(DC, P).T,
        "W2": np.asarray(L0_attn_W2).reshape(DC, P, D).transpose(1, 0, 2),
        "b2": np.asarray(L0_attn_b2).reshape(DC, P).T,
        "gateT": np.asarray(L0_ffn_gate_w).reshape(E, DC, P).transpose(2, 1, 0),
        "experts": np.concatenate(turned + [down], axis=2),
    }
    arrays.update(constants())
    arrays = {k: np.ascontiguousarray(v) for k, v in arrays.items()}
    nc = bacc.Bacc("TRN2", target_bir_lowering=False, num_devices=1)
    aps = {k: nc.dram_tensor(f"in_{k}", v.shape, mybir.dt.from_np(v.dtype), kind="ExternalInput").ap() for k, v in arrays.items()}
    out = nc.dram_tensor("out_y", (T, D), F32, kind="ExternalOutput").ap()
    build(nc, out=out, **aps)
    r = run_bass_kernel_spmd(nc, [{f"in_{k}": v for k, v in arrays.items()}], core_ids=[0])
    return r.results[0]["out_y"].reshape(B, L, D)
```

```python
from contextlib import ExitStack

import numpy as np

import concourse.bass as bass
from concourse import mybir

P = 128
B, L, D = 2, 2048, 256
T = B * L
NI = T // P
NB = NI // B
FO = 64
N1, N2 = L // P, P
GD = P // N1
LG = 8
LOADS = D // GD // LG
FILLS = D // GD // 2
CH = 32
NCH = D // CH
E, H, K = 8, 512, 2
CAP = int(1.25 * T / E)
RT = CAP // P
HALF = CAP // 2
ROWS = E * CAP
YS = 8
ZR = 4
DC, HC = D // P, H // P
WPART = DC * H
WSCALE = 16.0
EPS = 1e-5
OUT_OF_RANGE = 32768.0

F32 = mybir.dt.float32
F16 = mybir.dt.float16
U32 = mybir.dt.uint32
ALU = mybir.AluOpType
ACT = mybir.ActivationFunctionType
X = mybir.AxisListType.X


def constants():
    f = np.float32
    c = {}
    pos = np.arange(L, dtype=f)[:, None]
    div = np.exp(np.arange(0, FO, 2, dtype=f) * f(-np.log(f(10000.0)) / f(FO)))
    ang = (pos * div).astype(f)
    pe = np.zeros((L, FO), f)
    pe[:, 0::2] = np.sin(ang)
    pe[:, 1::2] = np.cos(ang)
    c["posT"] = np.ascontiguousarray(pe.T)
    n1 = np.arange(N1)[:, None]
    k1 = np.arange(N1)[None, :]
    th = 2 * np.pi * n1 * (k1 + 0.25) / N1
    across = np.zeros((GD, N1, N1, 2, GD))
    for d in range(GD):
        across[d, :, :, 0, d] = np.cos(th)
        across[d, :, :, 1, d] = -np.sin(th)
    c["across"] = across.reshape(P, 2 * N1 * GD).astype(f)
    n2 = np.arange(N2, dtype=np.float64)
    within = np.zeros((N1, P, 6, P))
    for k in range(N1):
        ph = 2 * np.pi * np.outer(n2, k + 0.25 + N1 * n2) / L
        within[k, :, 0] = np.cos(ph)
        within[k, :, 1] = -np.sin(ph)
        within[k, :, 2] = np.sin(ph)
        within[k, :, 3] = np.cos(ph).T / L
        within[k, :, 4] = np.sin(ph).T / L
        within[k, :, 5] = -np.sin(ph).T / L
    c["within"] = within.reshape(N1, P, 6 * P).astype(f)
    back = np.zeros((4, N1, 2, 2, N1, 4, 2))
    for q in range(4):
        for h in range(2):
            back[q, :, 0, h, :, q, h] = np.cos(th).T
            back[q, :, 1, h, :, q, h] = -np.sin(th).T
    c["back"] = back.reshape(P, 2 * P).astype(f)
    c["ident"] = np.eye(P, dtype=f)
    c["below"] = np.triu(np.ones((P, P)), 1).astype(f)
    rows = np.zeros((P, K * E * NB + E + E))
    mask = np.ones((K * E, NB))
    mask[:, 0] = 0
    rows[:, 0:K * E * NB] = mask.reshape(-1)
    rows[:, K * E * NB:K * E * NB + E] = np.arange(E) * CAP
    rows[:, K * E * NB + E:] = E - np.arange(E)
    c["rows"] = rows.astype(f)
    return c


def build(nc, xT, xN, W1, b1, W2, b2, gateT, experts, posT, across, within, back, ident, below, rows, out):
    fil_dram = nc.dram_tensor("fil_dram", (D, L), F32, kind="Internal").ap()
    xg_dram = [nc.dram_tensor(f"xg{k}_dram", (ROWS, D), F32, kind="Internal").ap() for k in range(K)]
    y_dram = [nc.dram_tensor(f"y{k}_dram", (ROWS, D), F32, kind="Internal").ap() for k in range(K)]

    ctx = ExitStack()
    with ctx:
        def sem(name):
            return ctx.enter_context(nc.semaphore(name))

        def sb(stack, name, shape, dt=F32):
            return stack.enter_context(nc.sbuf_tensor(name, shape, dt))

        xn = sb(ctx, "xn", [P, NI, D])
        c_ident = sb(ctx, "c_ident", [P, P])
        c_below = sb(ctx, "c_below", [P, P])
        c_rows = sb(ctx, "c_rows", [P, K * E * NB + 2 * E])
        c_ones = sb(ctx, "c_ones", [P, P])
        c_gate = sb(ctx, "c_gate", [P, DC, E])
        stats = sb(ctx, "stats", [P, NI, 6])
        lnt = sb(ctx, "lnt", [P, 8, NI])
        w_top = sb(ctx, "w_top", [P, K, NI])
        idx_put = sb(ctx, "idx_put", [P, K, NI], U32)
        idx_get = sb(ctx, "idx_get", [P, K, NI], U32)

        conv = ExitStack()
        c_across = sb(conv, "c_across", [P, 2 * N1 * GD])
        c_back = sb(conv, "c_back", [P, 2, P])
        ring = [sb(conv, f"ring{s}", [P, LG, N2]) for s in range(2)]
        bufa = sb(conv, "bufa", [P, 2 * N1 * D])
        x1b = sb(conv, "x1b", [P, 2 * N1, D])
        mats = [sb(conv, f"mats{s}", [P, 6, P]) for s in range(4)]
        fhat = sb(conv, "fhat", [P, N1, 2, D])
        prod = [sb(conv, f"prod{s}", [P, 2, 2, D]) for s in range(2)]
        yhat = [sb(conv, f"yhat{s}", [P, 2, D]) for s in range(2)]
        zt = [sb(conv, f"zt{s}", [P, CH * 32]) for s in range(2)]
        w1 = sb(conv, "w1", [FO, D])
        w2 = sb(conv, "w2", [P, DC, D])
        bias = sb(conv, "bias", [P, 2, DC])
        zeros = sb(conv, "zeros", [P, ZR * D])
        xst = [sb(conv, f"xst{s}", [P, D]) for s in range(4)]
        xts = [sb(conv, f"xts{s}", [P, 2, DC, P]) for s in range(2)]
        rt = sb(conv, "rt", [P, 8, NB * E])
        small = sb(conv, "small", [P, 8, NB])
        oh = sb(conv, "oh", [P, K, E, NB])
        scan = sb(conv, "scan", [P, K, E, NB])
        rk = sb(conv, "rk", [P, K, E, NB])
        red = sb(conv, "red", [P, 6, K, NB])
        tot = sb(conv, "tot", [P, B, K * E])
        base = sb(conv, "base", [P, K * E])
        x1f = bufa.rearrange("p (k d) -> p k d", k=2 * N1)
        z = bufa.rearrange("p (c k) -> p c k", k=2 * N1)
        fT = bufa[:, 0:DC * L].rearrange("p (c l) -> p c l", c=DC)
        early = fhat.rearrange("p k r d -> p (k r d)")
        hT = early[:, 0:DC * L].rearrange("p (c l) -> p c l", c=DC)
        pos = early[0:FO, DC * L:DC * L + L]
        conv.close()

        moe = ExitStack()
        wh = sb(moe, "wh", [P, E, 3 * WPART], F16)
        wl = sb(moe, "wl", [P, E, 3 * WPART], F16)
        yg = [sb(moe, f"yg{s}", [P, D]) for s in range(YS)]
        run = ExitStack()
        wst = [sb(run, f"wst{s}", [P, WPART]) for s in range(2)]
        xg = [sb(run, f"xg{s}", [P, RT, D]) for s in range(2)]
        xth = [sb(run, f"xth{s}", [P, DC, CAP], F16) for s in range(2)]
        xtl = [sb(run, f"xtl{s}", [P, DC, CAP], F16) for s in range(2)]
        ah = [sb(run, f"ah{s}", [P, HC, CAP], F16) for s in range(2)]
        al = [sb(run, f"al{s}", [P, HC, CAP], F16) for s in range(2)]
        s32 = [sb(run, f"s32_{s}", [P, HALF]) for s in range(2)]
        a32 = [sb(run, f"a32_{s}", [P, HALF]) for s in range(2)]
        ysb = [sb(run, f"ysb{s}", [P, RT, D]) for s in range(2)]
        run.close()
        fin = [sb(moe, f"fin{u}", [P, YS, D]) for u in range(2)]
        moe.close()

        ps = ctx.enter_context(nc.psum_tensor("ps", [P, 8, 512], F32))

        in_filter, in_across, in_back, in_xn, in_const = (sem(n) for n in ("in_filter", "in_across", "in_back", "in_xn", "in_const"))
        in_ring = [sem(f"in_ring{s}") for s in range(2)]
        in_mats = [sem(f"in_mats{s}") for s in range(4)]
        fil_stored = [sem(f"fil_stored{c}") for c in range(DC)]
        zero_stored = sem("zero_stored")
        put_done = [sem(f"put_done{k}") for k in range(K)]
        in_xg = [sem(f"in_xg{s}") for s in range(2)]
        in_w = [sem(f"in_w{s}") for s in range(2)]
        y_stored = [sem(f"y_stored{s}") for s in range(2)]
        in_yg = [sem(f"in_yg{s}") for s in range(YS)]
        out_stored = sem("out_stored")
        h_full, h_done, f_full, f_done, zeros_set = (sem(n) for n in ("h_full", "h_done", "f_full", "f_done", "zeros_set"))
        x1_full, x1_done = sem("x1_full"), sem("x1_done")
        fwd_full, fhat_done, prod_done, y_ready = (sem(n) for n in ("fwd_full", "fhat_done", "prod_done", "y_ready"))
        z_full, z_done = sem("z_full"), sem("z_done")
        zt_done, back_full, added = sem("zt_done"), sem("back_full"), sem("added")
        st_done, ln_step, sq_done = sem("st_done"), sem("ln_step"), sem("sq_done")
        xst_done, xst_kept, xst_turned, xts_done, logits_full = (sem(n) for n in ("xst_done", "xst_kept", "xst_turned", "xts_done", "logits_full"))
        r_step, e_ready, e_done, tot_ready, base_full, idx_ready = (sem(n) for n in ("r_step", "e_ready", "e_done", "tot_ready", "base_full", "idx_ready"))
        xt_full, xth_done, xtl_done = sem("xt_full"), sem("xth_done"), sem("xtl_done")
        wh_done, wl_done = sem("wh_done"), sem("wl_done")
        gu_full, s_done, a_done, ah_done, al_done = (sem(n) for n in ("gu_full", "s_done", "a_done", "ah_done", "al_done"))
        y_full, y_done = sem("y_full"), sem("y_done")
        yg_used = sem("yg_used")
        fin_step, fin_var, fin_sq, fin_scale, fin_done = (sem(n) for n in ("fin_step", "fin_var", "fin_sq", "fin_scale", "fin_done"))

        XT_PER = (RT + 1) // 2
        Q_PER = 2 * HC
        TURNS_AT = {1: (0, 1), 3: (2,)}
        src_x = xT.rearrange("b (s g p) (n m) -> b s (p n) g m", s=LOADS, g=LG, n=N1)
        src_f = fil_dram.rearrange("(s g p) (n m) -> s (p n) g m", s=LOADS, g=LG, n=N1)
        xg_v = [t.rearrange("(n j p) d -> n p j d", j=RT, p=P) for t in xg_dram]
        y_v = [t.rearrange("(n j p) d -> n p j d", j=RT, p=P) for t in y_dram]
        xg_zero = [t.rearrange("(p n r) d -> n p (r d)", p=P, r=ZR) for t in xg_dram]
        xn_in = xN.rearrange("(b p i) d -> b p (i d)", b=B, p=P)
        out_v = out.rearrange("(b p i) d -> b p i d", b=B, p=P)

        block = ctx.enter_context(nc.Block())

        @block.sync
        def _(sp):
            for dst, src in ((w1[:, :], W1), (bias[:, 0, :], b1), (pos[:, :], posT), (w2[:, :, :], W2), (bias[:, 1, :], b2)):
                sp.dma_start(dst, src).then_inc(in_filter, 16)
            sp.dma_start(c_across[:, :], across).then_inc(in_across, 16)

            def load_ring(m, l2, s, src):
                sp.wait_ge(x1_full, 4 * (LOADS * m + 2 * l2 + s) + 4)
                sp.dma_start(ring[s][:, :, :], src[2 * l2 + s]).then_inc(in_ring[s], 16)

            def load_mats(s, k, parts=6):
                sp.dma_start(mats[s][:, 0:parts, :], within[k].rearrange("p (m c) -> p m c", m=6)[:, 0:parts]).then_inc(in_mats[s], 16)

            for l2 in range(LOADS // 2):
                for s in range(2):
                    load_ring(0, l2, s, src_x[0])
            for s in range(4):
                load_mats(s, s, 3)
            for l2 in range(LOADS // 2):
                sp.wait_ge(fil_stored[l2], 16)
                for s in range(2):
                    load_ring(1, l2, s, src_f)
            with sp.Fori(1, N1 // 4) as k4:
                for s in range(4):
                    sp.wait_ge(fwd_full, 4 * k4 + s - 3)
                    load_mats(s, 4 * k4 + s, 3)
            for s in range(4):
                sp.wait_ge(fwd_full, N1 + s - 3)
                load_mats(s, s)
            for s in range(2):
                load_ring(2, 0, s, src_x[1])
            with sp.Fori(1, N1 // 4) as k4:
                for s in range(4):
                    sp.wait_ge(z_full, 4 * k4 + s - 3)
                    load_mats(s, 4 * k4 + s)
            for s in range(2):
                load_ring(2, 1, s, src_x[1])
            with sp.Fori(0, N1 // 4) as k4:
                for s in range(4):
                    sp.wait_ge(z_full, N1 + 4 * k4 + s - 3)
                    load_mats(s, 4 * k4 + s)

            def load_rows(s, k, e):
                n = k * E + e
                sp.wait_ge(xt_full, XT_PER * (n + 1))
                sp.dma_start(xg[s][:, :, :], xg_v[k][e]).then_inc(in_xg[s], 16)

            def load_weights(e, parity):
                for j in range(3):
                    s = (3 * parity + j) % 2
                    sp.wait_ge(wl_done, 3 * e + j + 1)
                    sp.dma_start(wst[s][:, :], experts[e, :, j * WPART:(j + 1) * WPART]).then_inc(in_w[s], 16)

            def store_y(s, k, e):
                n = k * E + e
                sp.wait_ge(y_done, 2 + RT * (n + 1))
                sp.dma_start(y_v[k][e], ysb[s][:, :, :]).then_inc(y_stored[s], 16)

            sp.wait_ge(idx_ready, 2)
            load_weights(0, 0)
            sp.wait_ge(put_done[0], 16 * NI)
            load_rows(0, 0, 0)
            load_rows(1, 0, 1)
            load_rows(0, 0, 2)
            load_weights(1, 1)
            with sp.Fori(0, (E - 4) // 2) as e2:
                e = 2 * e2 + 1
                for s in (1, 0):
                    load_rows(s, 0, e + (1 - s) + 2)
                    load_weights(e + (1 - s) + 1, 1 - s)
                    store_y(1 - s, 0, e + (1 - s) - 1)
            load_rows(1, 0, E - 1)
            load_weights(E - 2, 0)
            store_y(0, 0, E - 4)
            sp.wait_ge(put_done[1], 16 * NI)
            load_rows(0, 1, 0)
            load_weights(E - 1, 1)
            store_y(1, 0, E - 3)
            load_rows(1, 1, 1)
            store_y(0, 0, E - 2)
            load_rows(0, 1, 2)
            store_y(1, 0, E - 1)
            with sp.Fori(0, (E - 4) // 2) as e2:
                e = 2 * e2 + 1
                for s in (1, 0):
                    load_rows(s, 1, e + (1 - s) + 2)
                    store_y(1 - s, 1, e + (1 - s) - 1)
            load_rows(1, 1, E - 1)
            for e in range(E - 4, E):
                store_y(e % 2, 1, e)
            for b in range(B):
                with sp.Fori(0, NB // 4) as g:
                    sp.wait_ge(fin_done, 2 * YS + b * NB + 4 * (g + 1))
                    sp.dma_start(out_v[b, :, bass.ds(4 * g, 4), :], xn[:, bass.ds(b * NB + 4 * g, 4), :]).then_inc(out_stored, 16)
            sp.wait_ge(out_stored, 16 * (NI // 4))

        @block.gpsimd
        def _(pool):
            nc.gpsimd.memset(zeros[:, :], 0.0).then_inc(zeros_set, 1)
            nc.gpsimd.memset(c_ones[:, :], 1.0).then_inc(zeros_set, 1)
            pool.wait_ge(zeros_set, 2)
            pool.wait_ge(fwd_full, 4)
            for b in range(B):
                pool.dma_start(xn[:, b * NB:(b + 1) * NB, :].rearrange("p i d -> p (i d)"), xn_in[b]).then_inc(in_xn, 16)
            for k in range(K):
                with pool.Fori(0, ROWS // P // ZR) as n:
                    pool.wait_ge(z_full, k * N1 + n + 1)
                    pool.dma_start(xg_zero[k][n], zeros[:, :]).then_inc(zero_stored, 16)
            pool.wait_ge(zero_stored, 16 * K * (ROWS // P // ZR))
            for b in range(B):
                pool.wait_ge(xst_kept, NB * (b + 1))
                pool.wait_ge(idx_ready, b + 1)
                for k in range(K):
                    for i in range(b * NB, (b + 1) * NB):
                        nc.gpsimd.indirect_dma_start(
                            xg_dram[k][:, :], bass.IndirectOffsetOnAxis(ap=idx_put[:, k, i:i + 1], axis=0), xn[:, i, :], None,
                            bounds_check=ROWS - 1, oob_is_err=False).then_inc(put_done[k], 16)
            pool.sem_inc(yg_used, YS)
            for k in range(K):
                for s in range(2):
                    pool.wait_ge(y_stored[s], 16 * (E // 2) * (k + 1) + 16)
                for i in range(NI):
                    pool.wait_ge(yg_used, k * NI + i + 1)
                    nc.gpsimd.indirect_dma_start(
                        yg[i % YS][:, :], None, y_dram[k][:, :],
                        bass.IndirectOffsetOnAxis(ap=idx_get[:, k, i:i + 1], axis=0)).then_inc(in_yg[i % YS], 16)

        @block.scalar
        def _(act):
            act.sem_inc(x1_done, 4)
            act.sem_inc(z_done, 4)
            act.sem_inc(y_done, 2)
            act.sem_inc(fhat_done, 2)
            act.sem_inc(fin_done, 2 * YS)
            for s in range(2):
                act.sem_inc(y_stored[s], 16)
            act.wait_ge(in_filter, 80)
            for n in range(DC * 4):
                act.wait_ge(h_full, n + 1)
                nc.scalar.activation(hT[:, n // 4, (n % 4) * 512:(n % 4 + 1) * 512], ps[:, n % 4, :], ACT.Gelu,
                                     bias=bias[:, 0, n // 4:n // 4 + 1]).then_inc(h_done, 1)
            for n in range(DC * 4):
                act.wait_ge(f_full, n + 1)
                nc.scalar.activation(fT[:, n // 4, (n % 4) * 512:(n % 4 + 1) * 512], ps[:, 4 + n % 4, :], ACT.Identity,
                                     bias=bias[:, 1, n // 4:n // 4 + 1]).then_inc(f_done, 1)
                if n % 4 == 3:
                    act.wait_ge(f_done, n + 1)
                    act.dma_start(fil_dram[(n // 4) * P:(n // 4 + 1) * P, :], fT[:, n // 4, :]).then_inc(fil_stored[n // 4], 16)

            act.dma_start(c_back[:, :, :], back.rearrange("p (h m) -> p h m", h=2)).then_inc(in_back, 16)
            for dst, src in ((c_ident[:, :], ident), (c_below[:, :], below), (c_rows[:, :], rows), (c_gate[:, :, :], gateT)):
                act.dma_start(dst, src).then_inc(in_const, 16)

            def keep_x1(m, buf):
                with act.Fori(0, FILLS // 4) as j4:
                    for s in range(4):
                        act.wait_ge(x1_full, 8 + FILLS * m + 4 * j4 + s + 1)
                        nc.scalar.activation(
                            buf[:, :, bass.ds(8 * GD * j4 + s * 2 * GD, 2 * GD)].rearrange("p k (g d) -> p k g d", g=2),
                            ps[:, s, :].rearrange("p (g k d) -> p k g d", g=2, d=GD), ACT.Copy).then_inc(x1_done, 1)

            zv = z.rearrange("p c k -> p k c")

            def keep_z(b, k, s):
                act.wait_ge(z_full, b * N1 + k + 1)
                nc.scalar.activation(zv[:, bass.ds(2 * k, 2), :], ps[:, 4 + s, :].rearrange("p (r c) -> p r c", r=2),
                                     ACT.Copy).then_inc(z_done, 1)

            def keep_turned(b, g):
                for s in range(2):
                    act.wait_ge(xst_turned, 4 + b * NB + 4 * g + 2 * s + 2)
                    nc.scalar.activation(xts[s][:, :, :, :].rearrange("p t c r -> p (t c r)"), ps[:, 2 + s, :], ACT.Copy).then_inc(xts_done, 1)

            def deviation(b):
                act.wait_ge(ln_step, 8 * b + 6)
                nc.scalar.activation(lnt[:, 5, b * NB:(b + 1) * NB], lnt[:, 3, b * NB:(b + 1) * NB], ACT.Sqrt).then_inc(sq_done, 1)

            def exps(b):
                act.wait_ge(e_ready, b + 1)
                nc.scalar.activation(rt[:, 2, :], rt[:, 1, :], ACT.Exp).then_inc(e_done, 1)

            keep_x1(0, x1b)
            for c in range(DC):
                act.wait_ge(fil_stored[c], 16)
            keep_x1(1, x1f)
            with act.Fori(0, N1 // 2) as k2:
                for s in range(2):
                    k = 2 * k2 + s
                    act.wait_ge(fwd_full, k + 1)
                    nc.scalar.activation(fhat[:, bass.ds(k, 1), :, :].rearrange("p a r d -> p (a r d)"), ps[:, s, :],
                                         ACT.Copy).then_inc(fhat_done, 1)
            with act.Fori(0, N1 // 2) as k2:
                for s in range(2):
                    keep_z(0, 2 * k2 + s, s)
            keep_x1(2, x1b)
            deviation(0)
            with act.Fori(0, N1 // 4 - 1) as k4:
                for s in range(4):
                    keep_z(1, 4 * k4 + s, s % 2)
                keep_turned(0, k4)
            keep_z(1, N1 - 4, 0)
            keep_turned(0, NB // 4 - 1)
            keep_z(1, N1 - 3, 1)
            exps(0)
            keep_z(1, N1 - 2, 0)
            keep_z(1, N1 - 1, 1)
            deviation(1)
            with act.Fori(0, NB // 4) as g:
                keep_turned(1, g)
            exps(1)

            def turn_hi(n, s, j):
                w = 2 if 2 * j + 1 < RT else 1
                act.wait_ge(xt_full, 2 * XT_PER + XT_PER * n + j + 1)
                nc.scalar.activation(
                    xth[s][:, :, 2 * j * P:(2 * j + w) * P].rearrange("p c (t r) -> p t c r", t=w),
                    ps[:, 4 + j % 2, 0:w * D].rearrange("p (t c r) -> p t c r", t=w, c=DC), ACT.Copy).then_inc(xth_done, 1)

            def weights_hi(e, parity, j):
                s = (3 * parity + j) % 2
                act.wait_ge(in_w[s], 24 * (e - parity) + 16 * ((3 * parity + j) // 2 + 1))
                nc.scalar.activation(wh[:, bass.ds(e, 1), j * WPART:(j + 1) * WPART],
                                     wst[s][:, :].unsqueeze(1), ACT.Copy, scale=WSCALE).then_inc(wh_done, 1)

            def a_hi(n, s, j):
                act.wait_ge(a_done, 2 + Q_PER * n + j + 1)
                nc.scalar.activation(ah[s][:, j // 2, (j % 2) * HALF:(j % 2 + 1) * HALF], a32[j % 2][:, :],
                                     ACT.Copy).then_inc(ah_done, 1)

            def keep_y(n, s, t):
                if t == 0:
                    act.wait_ge(y_stored[s], 8 * (n - s) + 16)
                act.wait_ge(y_full, RT * n + t + 1)
                nc.scalar.activation(ysb[s][:, t, :], ps[:, 6 + (RT * s + t) % 2, 0:D], ACT.Copy, scale=1.0 / WSCALE).then_inc(y_done, 1)

            def expert(n, s, split=False, turn=True, last_rows=True):
                for j in range(Q_PER):
                    act.wait_ge(gu_full, Q_PER * n + j + 1)
                    act.wait_ge(a_done, Q_PER * n + j + 1)
                    nc.scalar.activation(s32[j % 2][:, :], ps[:, 2 * (j % 2), 0:HALF], ACT.Silu, scale=1.0 / WSCALE).then_inc(s_done, 1)
                    if j:
                        a_hi(n, s, j - 1)
                    if turn and j in TURNS_AT:
                        for t in TURNS_AT[j]:
                            turn_hi(n + 1, 1 - s, t)
                    if last_rows and 2 <= j < 2 + RT:
                        keep_y(n - 1, 1 - s, j - 2)
                    if split and j in (2, 4, 6):
                        weights_hi(n + 1, 1 - s, j // 2 - 1)
                a_hi(n, s, Q_PER - 1)

            for j in range(3):
                weights_hi(0, 0, j)
            for j in range(XT_PER):
                turn_hi(0, 0, j)
            expert(0, 0, split=True, last_rows=False)
            with act.Fori(0, (E - 2) // 2) as n2:
                n = 2 * n2 + 1
                expert(n, 1, split=True)
                expert(n + 1, 0, split=True)
            expert(E - 1, 1)
            expert(E, 0)
            with act.Fori(0, (E - 2) // 2) as n2:
                n = 2 * n2 + E + 1
                expert(n, 1)
                expert(n + 1, 0)
            expert(2 * E - 1, 1, turn=False)
            for t in range(RT):
                keep_y(2 * E - 1, 1, t)
            with act.Fori(0, NI // YS // 2) as g2:
                for u in range(2):
                    g = 2 * g2 + u
                    r = slice(u * YS, (u + 1) * YS)
                    act.wait_ge(fin_var, g + 1)
                    nc.scalar.activation(lnt[:, 5, r], lnt[:, 3, r], ACT.Sqrt).then_inc(fin_sq, 1)
                    act.wait_ge(fin_scale, g + 1)
                    for j in range(YS):
                        nc.scalar.activation(xn[:, bass.ds(YS * g + j, 1), :].rearrange("p a d -> p (a d)"), fin[u][:, j, :], ACT.Identity,
                                             bias=lnt[:, 7, u * YS + j:u * YS + j + 1],
                                             scale=lnt[:, 6, u * YS + j:u * YS + j + 1]).then_inc(fin_done, 1)

        @block.tensor
        def _(pe):
            pe.sem_inc(x1_full, 8)
            pe.sem_inc(xst_turned, 4)
            pe.sem_inc(xt_full, 2 * XT_PER)
            mm = nc.tensor.matmul
            pe.wait_ge(in_filter, 80)
            for n in range(DC * 4):
                if n >= 4:
                    pe.wait_ge(h_done, n - 3)
                mm(ps[:, n % 4, :], w1[:, (n // 4) * P:(n // 4 + 1) * P], pos[:, (n % 4) * 512:(n % 4 + 1) * 512],
                   start=True, stop=True).then_inc(h_full, 1)
            for n in range(DC * 4):
                pe.wait_ge(h_done, DC * 4)
                if n >= 4:
                    pe.wait_ge(f_done, n - 3)
                for c in range(DC):
                    last = mm(ps[:, 4 + n % 4, :], w2[:, c, (n // 4) * P:(n // 4 + 1) * P],
                              hT[:, c, (n % 4) * 512:(n % 4 + 1) * 512], start=(c == 0), stop=(c == DC - 1))
                last.then_inc(f_full, 1)

            def go_across(m):
                with pe.Fori(0, LOADS // 2) as l2:
                    for s in range(2):
                        pe.wait_ge(in_ring[s], 16 * (LOADS // 2 * m + l2 + 1))
                        for j in range(4):
                            pe.wait_ge(x1_done, FILLS * m + 8 * l2 + 4 * s + j + 1)
                            for g in range(2):
                                last = mm(ps[:, j, g * 256:(g + 1) * 256], ring[s][:, 2 * j + g, :], c_across[:, :],
                                          start=True, stop=True)
                            last.then_inc(x1_full, 1)

            def forward(m, k, buf, s, ms):
                pe.wait_ge(in_mats[ms], 4 * (N1 * m + k - ms) + 16)
                re = buf[:, bass.ds(2 * k, 1), :].rearrange("p a c -> p (a c)")
                im = buf[:, bass.ds(2 * k + 1, 1), :].rearrange("p a c -> p (a c)")
                w = mats[ms]
                mm(ps[:, s, 0:D], w[:, 0, :], re, start=True, stop=False)
                mm(ps[:, s, 0:D], w[:, 2, :], im, start=False, stop=True)
                mm(ps[:, s, D:2 * D], w[:, 1, :], re, start=True, stop=False)
                mm(ps[:, s, D:2 * D], w[:, 0, :], im, start=False, stop=True).then_inc(fwd_full, 1)

            def forward_x(b, k, s, ms):
                pe.wait_ge(prod_done, 2 * (N1 * b + k) + 2)
                forward(1 + b, k, x1b, s, ms)

            def inverse(b, k, s, ms):
                n = N1 * b + k
                pe.wait_ge(y_ready, 4 + 2 * n + 2)
                pe.wait_ge(z_done, n + 3)
                w = mats[ms]
                mm(ps[:, 4 + s, 0:D], w[:, 3, :], yhat[s][:, 0, :], start=True, stop=False)
                mm(ps[:, 4 + s, 0:D], w[:, 5, :], yhat[s][:, 1, :], start=False, stop=True)
                mm(ps[:, 4 + s, D:2 * D], w[:, 4, :], yhat[s][:, 0, :], start=True, stop=False)
                mm(ps[:, 4 + s, D:2 * D], w[:, 3, :], yhat[s][:, 1, :], start=False, stop=True).then_inc(z_full, 1)

            def go_back(b):
                with pe.Fori(0, NCH // 2) as c2:
                    for s in range(2):
                        pe.wait_ge(zt_done, NCH * b + 2 * c2 + s + 1)
                        zs = zt[s].rearrange("p (d h i) -> p h d i", h=2, i=NB)
                        for h in range(2):
                            last = mm(ps[:, 6 + s, :], c_back[:, h, :], zs[:, h], start=(h == 0), stop=(h == 1))
                        last.then_inc(back_full, 1)

            def gate_columns(b, g):
                i = b * NB + 4 * g
                for s in range(4):
                    pe.wait_ge(xst_done, i + s + 1)
                    for c in range(DC):
                        o = (s % 2) * D + c * P
                        last = nc.tensor.transpose(ps[:, 2 + s // 2, o:o + P], xst[s][:, c * P:(c + 1) * P], c_ident[:, :])
                    last.then_inc(xst_turned, 1)
                for s in range(4):
                    if s % 2 == 0:
                        pe.wait_ge(xts_done, b * (NB // 2) + 2 * g + s // 2 + 1)
                    for c in range(DC):
                        last = mm(ps[:, 6, bass.ds((i + s) * E, E)], xts[s // 2][:, s % 2, c, :], c_gate[:, c, :],
                                  start=(c == 0), stop=(c == DC - 1), skip_group_check=True)
                    last.then_inc(logits_full, 1)

            def ranks_base(b):
                pe.wait_ge(tot_ready, b + 1)
                last = mm(ps[:, 7, 0:K * E], c_below[:, :], tot[:, b, :], start=True, stop=(b == 0))
                if b:
                    last = mm(ps[:, 7, 0:K * E], c_ones[:, :], tot[:, 0, :], start=False, stop=True)
                last.then_inc(base_full, 1)

            pe.wait_ge(in_across, 16)
            go_across(0)
            go_across(1)
            pe.wait_ge(x1_done, 4 + 2 * FILLS)
            with pe.Fori(0, N1 // 4) as k4:
                for s in range(4):
                    pe.wait_ge(fhat_done, 4 * k4 + s + 1)
                    forward(0, 4 * k4 + s, x1f, s % 2, s)
            pe.wait_ge(fhat_done, 2 + N1)
            pe.wait_ge(in_back, 16)
            for b in range(B):
                pe.wait_ge(x1_done, 4 + (2 + b) * FILLS)
                forward_x(b, 0, 0, 0)
                with pe.Fori(0, N1 // 4 - 1) as k4:
                    for j in range(4):
                        forward_x(b, 4 * k4 + j + 1, (j + 1) % 2, (j + 1) % 4)
                        inverse(b, 4 * k4 + j, j % 2, j)
                    if b == 1:
                        gate_columns(0, k4)
                for k in range(N1 - 4, N1):
                    if k + 1 < N1:
                        forward_x(b, k + 1, (k + 1) % 2, (k + 1) % 4)
                    inverse(b, k, k % 2, k % 4)
                    if b == 1 and k == N1 - 4:
                        gate_columns(0, NB // 4 - 1)
                if b == 1:
                    ranks_base(0)
                go_back(b)
                if b == 0:
                    pe.wait_ge(in_const, 64)
                    go_across(2)
            with pe.Fori(0, NB // 4) as g:
                gate_columns(1, g)
            ranks_base(1)

            def turn(n, s, j):
                if j == 0:
                    pe.wait_ge(in_xg[s], 8 * (n - s) + 16)
                if j == 2:
                    pe.wait_ge(xtl_done, XT_PER * n + 1)
                for t in range(2 * j, min(2 * j + 2, RT)):
                    for c in range(DC):
                        o = (t % 2) * D + c * P
                        last = nc.tensor.transpose(ps[:, 4 + j % 2, o:o + P], xg[s][:, t, c * P:(c + 1) * P], c_ident[:, :])
                last.then_inc(xt_full, 1)

            def split_mm(o, whi, wlo, xhi, xlo, start, stop):
                mm(o, whi, xhi, start=start, stop=False)
                mm(o, whi, xlo, start=False, stop=False)
                return mm(o, wlo, xhi, start=False, stop=stop)

            def wslice(w, e, off, width):
                return w[:, bass.ds(e, 1), off:off + width].rearrange("p a c -> p (a c)")

            def down(n, e, s, t):
                pe.wait_ge(y_done, RT * n + t + 1)
                if t == 0:
                    pe.wait_ge(al_done, 2 + Q_PER * (n + 1))
                    pe.wait_ge(wl_done, 2 + 3 * (e + 1))
                for c in range(HC):
                    off = 2 * WPART + c * D
                    last = split_mm(ps[:, 6 + (RT * s + t) % 2, 0:D], ah[s][:, c, t * P:(t + 1) * P], al[s][:, c, t * P:(t + 1) * P],
                                    wslice(wh, e, off, D), wslice(wl, e, off, D), c == 0, c == HC - 1)
                last.then_inc(y_full, 1)

            def expert(n, e, s, turn_next=True, last_rows=True, last_e=None):
                pe.wait_ge(xtl_done, XT_PER * (n + 1))
                pe.wait_ge(wl_done, 2 + 3 * e + 2)
                for j in range(Q_PER):
                    pe.wait_ge(a_done, Q_PER * n + j + 1)
                    r = slice((j % 2) * HALF, (j % 2 + 1) * HALF)
                    for part in range(2):
                        for c in range(DC):
                            off = part * WPART + c * H + (j // 2) * P
                            last = split_mm(ps[:, 2 * (j % 2) + part, 0:HALF], wslice(wh, e, off, P), wslice(wl, e, off, P),
                                            xth[s][:, c, r], xtl[s][:, c, r], c == 0, c == DC - 1)
                    last.then_inc(gu_full, 1)
                    if turn_next:
                        for t in TURNS_AT.get(j + 1, ()):
                            turn(n + 1, 1 - s, t)
                    if last_rows and 1 <= j < 1 + RT:
                        down(n - 1, e - 1 if last_e is None else last_e, 1 - s, j - 1)

            for j in range(XT_PER):
                turn(0, 0, j)
            expert(0, 0, 0, last_rows=False)
            with pe.Fori(0, (E - 2) // 2) as e2:
                e = 2 * e2 + 1
                expert(e, e, 1)
                expert(e + 1, e + 1, 0)
            expert(E - 1, E - 1, 1)
            expert(E, 0, 0, last_e=E - 1)
            with pe.Fori(0, (E - 2) // 2) as e2:
                e = 2 * e2 + 1
                expert(E + e, e, 1)
                expert(E + e + 1, e + 1, 0)
            expert(2 * E - 1, E - 1, 1, turn_next=False)
            for t in range(RT):
                down(2 * E - 1, E - 1, 1, t)

        @block.vector
        def _(dve):
            v = nc.vector
            dve.sem_inc(prod_done, 4)
            dve.sem_inc(wl_done, 2)
            dve.sem_inc(a_done, 2)
            dve.sem_inc(y_ready, 4)
            dve.sem_inc(al_done, 2)

            def multiply(b, k, s):
                n = N1 * b + k
                dve.wait_ge(fwd_full, N1 + n + 1)
                dve.wait_ge(y_ready, 2 * n + 2)
                xs = ps[:, s, :].rearrange("p (r d) -> p r d", r=2)
                fs = fhat[:, bass.ds(k, 1), :, :].rearrange("p a r d -> p (a r) d")
                v.tensor_tensor(prod[s][:, 0], xs, fs, ALU.mult).then_inc(prod_done, 1)
                v.tensor_tensor(prod[s][:, 1], xs[:, ::-1, :], fs, ALU.mult).then_inc(prod_done, 1)
                dve.wait_ge(prod_done, 2 * n + 6)
                dve.wait_ge(z_done, n + 3)
                for w, op in ((0, ALU.subtract), (1, ALU.add)):
                    v.tensor_tensor(yhat[s][:, w, :], prod[s][:, w, 0], prod[s][:, w, 1], op).then_inc(y_ready, 1)

            def turn_back(b):
                dve.wait_ge(z_done, 4 + N1 * (b + 1))
                dve.wait_ge(in_xn, 32)
                for c in range(NCH + 2):
                    if c >= 2:
                        dve.wait_ge(back_full, NCH * b + c - 1)
                        dst = xn[:, b * NB:(b + 1) * NB, (c - 2) * CH:(c - 1) * CH].rearrange("p i d -> p d i")
                        v.tensor_tensor(dst, ps[:, 6 + c % 2, :].rearrange("p (d i) -> p d i", i=NB), dst, ALU.add).then_inc(added, 1)
                    if c < NCH:
                        v.transpose(zt[c % 2][:, :], z[:, c * CH:(c + 1) * CH, :].rearrange("p c k -> p (c k)")).then_inc(zt_done, 1)

            def norm_steps(st, lo, hi):
                r = lambda n: lnt[:, n, lo:hi]
                return [
                    lambda: v.tensor_tensor(r(0), st[:, :, 1], st[:, :, 4], ALU.add),
                    lambda: v.tensor_tensor(r(1), st[:, :, 1], st[:, :, 4], ALU.subtract),
                    lambda: v.tensor_tensor(r(2), st[:, :, 2], st[:, :, 5], ALU.add),
                    lambda: v.tensor_tensor(r(1), r(1), r(1), ALU.mult),
                    lambda: v.scalar_tensor_tensor(r(3), r(1), D / 4.0, r(2), ALU.mult, ALU.add),
                    lambda: v.tensor_scalar(r(3), r(3), 1.0 / D, EPS, ALU.mult, ALU.add),
                    lambda: v.tensor_scalar(r(4), r(0), 0.5, None, ALU.mult),
                ]

            def moments(b):
                lo, hi = b * NB, (b + 1) * NB
                dve.wait_ge(added, NCH * (b + 1))
                with dve.Fori(lo, hi) as i:
                    v.bn_stats(stats[:, bass.ds(i, 1), :].rearrange("p a c -> p (a c)"),
                               xn[:, bass.ds(i, 1), :].rearrange("p a c -> p (a c)")).then_inc(st_done, 1)
                dve.wait_ge(st_done, hi)
                for n, step in enumerate(norm_steps(stats[:, lo:hi], lo, hi)):
                    if n:
                        dve.wait_ge(ln_step, 8 * b + n)
                    step().then_inc(ln_step, 1)
                dve.wait_ge(sq_done, b + 1)
                v.reciprocal(lnt[:, 6, lo:hi], lnt[:, 5, lo:hi]).then_inc(ln_step, 1)
                dve.wait_ge(ln_step, 8 * (b + 1))

            def normalise(b, g):
                for keep in range(2):
                    for s in range(4):
                        i = b * NB + 4 * g + s
                        if keep == 0:
                            dve.wait_ge(xst_turned, i + 1)
                        else:
                            dve.wait_ge(xst_done, i + 1)
                        col = xn[:, bass.ds(i, 1), :].rearrange("p a c -> p (a c)")
                        v.tensor_scalar(col if keep else xst[s][:, :], col, lnt[:, 4, bass.ds(i, 1)], lnt[:, 6, bass.ds(i, 1)],
                                        ALU.subtract, ALU.mult).then_inc(xst_kept if keep else xst_done, 1)

            count = [0]

            def step(ins):
                ins.then_inc(r_step, 1)
                count[0] += 1
                dve.wait_ge(r_step, count[0])

            def ie(k):
                return rt[:, k, :].rearrange("p (i e) -> p i e", e=E)

            def over_e(ap):
                return ap.unsqueeze(2).to_broadcast([P, NB, E])

            def flat(t):
                return t.rearrange("p k e i -> p (k e i)")

            KEI = K * E * NB
            first_of = c_rows[:, KEI + E:KEI + 2 * E].unsqueeze(1).to_broadcast([P, NB, E])
            region = c_rows[:, KEI:KEI + E].unsqueeze(1).unsqueeze(3).to_broadcast([P, K, E, NB])

            def choose(b):
                dve.wait_ge(logits_full, NB * (b + 1))
                step(v.tensor_copy(rt[:, 0, :], ps[:, 6, b * NB * E:(b + 1) * NB * E]))
                step(v.tensor_reduce(small[:, 0, :], ie(0), X, ALU.max))
                v.tensor_tensor(ie(1), ie(0), over_e(small[:, 0, :]), ALU.subtract).then_inc(e_ready, 1)
                dve.wait_ge(e_done, b + 1)
                step(v.tensor_reduce(small[:, 1, :], ie(2), X, ALU.add))
                step(v.reciprocal(small[:, 2, :], small[:, 1, :]))
                step(v.tensor_tensor(ie(3), ie(2), over_e(small[:, 2, :]), ALU.mult))
                for k in range(K):
                    p_k, top = ie(3 + k), small[:, 3 + k, :]
                    step(v.tensor_reduce(top, p_k, X, ALU.max))
                    step(v.tensor_tensor(ie(5), p_k, over_e(top), ALU.is_equal))
                    step(v.tensor_tensor(ie(6), ie(5), first_of, ALU.mult))
                    step(v.tensor_reduce(small[:, 5, :], ie(6), X, ALU.max))
                    step(v.tensor_tensor(oh[:, k].rearrange("p e i -> p i e"), first_of, over_e(small[:, 5, :]), ALU.is_equal))
                    if k == 0:
                        step(v.scalar_tensor_tensor(ie(4), oh[:, 0].rearrange("p e i -> p i e"), -2.0, ie(3), ALU.mult, ALU.add))
                step(v.tensor_tensor_scan(flat(scan), c_rows[:, 0:KEI], flat(oh), 0.0, ALU.mult, ALU.add))
                v.tensor_copy(tot[:, b, :], scan[:, :, :, NB - 1].rearrange("p k e -> p (k e)")).then_inc(tot_ready, 1)
                step(v.tensor_tensor(small[:, 6, :], small[:, 3, :], small[:, 4, :], ALU.add))
                step(v.tensor_scalar(small[:, 6, :], small[:, 6, :], 1e-9, None, ALU.add))
                step(v.reciprocal(small[:, 7, :], small[:, 6, :]))
                step(v.tensor_tensor(rk[:, :], region, oh[:, :], ALU.mult))
                step(v.tensor_reduce(red[:, 1], rk[:, :].rearrange("p k e i -> p k i e"), X, ALU.add))

            def place(b):
                mine = slice(b * NB, (b + 1) * NB)
                dve.wait_ge(base_full, b + 1)
                step(v.tensor_copy(base[:, :], ps[:, 7, 0:K * E]))
                step(v.tensor_tensor(rk[:, :], scan[:, :],
                                     base[:, :].rearrange("p (k e) -> p k e", k=K).unsqueeze(3).to_broadcast([P, K, E, NB]), ALU.add))
                step(v.tensor_tensor(rk[:, :], rk[:, :], oh[:, :], ALU.mult))
                step(v.tensor_reduce(red[:, 0], rk[:, :].rearrange("p k e i -> p k i e"), X, ALU.add))
                step(v.tensor_scalar(red[:, 2], red[:, 0], float(CAP), None, ALU.is_le))
                step(v.scalar_tensor_tensor(red[:, 3], red[:, 0], -1.0, red[:, 1], ALU.add, ALU.add))
                step(v.tensor_tensor(red[:, 4], red[:, 3], red[:, 2], ALU.mult))
                step(v.tensor_scalar(red[:, 5], red[:, 2], -OUT_OF_RANGE, OUT_OF_RANGE, ALU.mult, ALU.add))
                step(v.tensor_tensor(red[:, 5], red[:, 5], red[:, 4], ALU.add))
                weigh(b)
                if b == B - 1:
                    dve.wait_ge(zero_stored, 16 * K * (ROWS // P // ZR))
                v.tensor_copy(idx_put[:, :, mine], red[:, 5]).then_inc(idx_ready, 1)

            def weigh(b):
                mine = slice(b * NB, (b + 1) * NB)
                step(v.tensor_copy(idx_get[:, :, mine], red[:, 4]))
                step(v.tensor_tensor(w_top[:, :, mine], small[:, 3:5, :], small[:, 7, :].unsqueeze(1).to_broadcast([P, K, NB]), ALU.mult))
                step(v.tensor_tensor(w_top[:, :, mine], w_top[:, :, mine], red[:, 2], ALU.mult))

            dve.wait_ge(fhat_done, 2 + N1)
            with dve.Fori(0, N1 // 2) as k2:
                for s in range(2):
                    multiply(0, 2 * k2 + s, s)
            turn_back(0)
            moments(0)
            dve.wait_ge(in_const, 64)
            with dve.Fori(0, N1 // 4 - 1) as k4:
                for s in range(4):
                    multiply(1, 4 * k4 + s, s % 2)
                normalise(0, k4)
            multiply(1, N1 - 4, 0)
            normalise(0, NB // 4 - 1)
            multiply(1, N1 - 3, 1)
            multiply(1, N1 - 2, 0)
            choose(0)
            multiply(1, N1 - 1, 1)
            place(0)
            turn_back(1)
            moments(1)
            with dve.Fori(0, NB // 4) as g:
                normalise(1, g)
            choose(1)
            place(1)
            def turn_lo(n, s, j):
                w = 2 if 2 * j + 1 < RT else 1
                dve.wait_ge(xth_done, XT_PER * n + j + 1)
                cols = lambda t: t[:, :, 2 * j * P:(2 * j + w) * P].rearrange("p c (t r) -> p t c r", t=w)
                v.tensor_tensor(cols(xtl[s]), ps[:, 4 + j % 2, 0:w * D].rearrange("p (t c r) -> p t c r", t=w, c=DC),
                                cols(xth[s]), ALU.subtract).then_inc(xtl_done, 1)

            def weights_lo(e, parity, j):
                s = (3 * parity + j) % 2
                dve.wait_ge(wh_done, 3 * e + j + 1)
                part = lambda t: t[:, bass.ds(e, 1), j * WPART:(j + 1) * WPART].rearrange("p a c -> p (a c)")
                v.scalar_tensor_tensor(part(wl), wst[s][:, :], WSCALE, part(wh), ALU.mult, ALU.subtract).then_inc(wl_done, 1)

            def a_lo(n, s, j):
                dve.wait_ge(ah_done, Q_PER * n + j + 1)
                r = slice((j % 2) * HALF, (j % 2 + 1) * HALF)
                v.tensor_tensor(al[s][:, j // 2, r], a32[j % 2][:, :], ah[s][:, j // 2, r], ALU.subtract).then_inc(al_done, 1)

            def expert(n, s, split=False, turn=True):
                for j in range(Q_PER):
                    dve.wait_ge(s_done, Q_PER * n + j + 1)
                    dve.wait_ge(al_done, Q_PER * n + j + 1)
                    v.scalar_tensor_tensor(a32[j % 2][:, :], ps[:, 2 * (j % 2) + 1, 0:HALF], 1.0 / WSCALE, s32[j % 2][:, :],
                                           ALU.mult, ALU.mult).then_inc(a_done, 1)
                    if j:
                        a_lo(n, s, j - 1)
                    if turn and j in TURNS_AT:
                        for t in TURNS_AT[j]:
                            turn_lo(n + 1, 1 - s, t)
                    if split and j in (3, 5, 7):
                        weights_lo(n + 1, 1 - s, (j - 3) // 2)
                a_lo(n, s, Q_PER - 1)

            def add_choice(k, i, round8, j, to=None):
                dve.wait_ge(in_yg[j], 16 * (k * (NI // YS) + round8 + 1))
                col = xn[:, bass.ds(i, 1), :].rearrange("p a c -> p (a c)")
                v.scalar_tensor_tensor(col if to is None else to, yg[j][:, :], w_top[:, k, bass.ds(i, 1)], col, ALU.mult, ALU.add).then_inc(yg_used, 1)

            def add_four(g, parity):
                for j in range(4):
                    add_choice(0, 8 * g + 4 * parity + j, g, 4 * parity + j)

            for j in range(3):
                weights_lo(0, 0, j)
            for j in range(XT_PER):
                turn_lo(0, 0, j)
            expert(0, 0, split=True)
            with dve.Fori(0, (E - 2) // 2) as e2:
                n = 2 * e2 + 1
                expert(n, 1, split=True)
                expert(n + 1, 0, split=True)
            expert(E - 1, 1)
            expert(E, 0)
            with dve.Fori(0, (E - 2) // 2) as e2:
                n = 2 * e2 + E + 1
                expert(n, 1)
                add_four(e2, 0)
                expert(n + 1, 0)
                add_four(e2, 1)
            expert(2 * E - 1, 1, turn=False)
            for parity in range(2):
                add_four(NI // YS - 1, parity)
            with dve.Fori(0, NI // YS // 2) as g2:
                for u in range(2):
                    g = 2 * g2 + u
                    st = stats[:, u * YS:(u + 1) * YS, :]
                    r = slice(u * YS, (u + 1) * YS)
                    steps = YS + 7
                    dve.wait_ge(fin_done, YS * g + YS)
                    for j in range(YS + 1):
                        if j < YS:
                            add_choice(1, YS * g + j, g, j, to=fin[u][:, j, :])
                        if j:
                            dve.wait_ge(yg_used, YS + NI + YS * g + j)
                            v.bn_stats(st[:, j - 1, :], fin[u][:, j - 1, :]).then_inc(fin_step, 1)
                    dve.wait_ge(fin_step, g * steps + YS)
                    for n, step_ in enumerate(norm_steps(st, u * YS, (u + 1) * YS)):
                        ins = step_()
                        if n == 5:
                            ins.then_inc(fin_var, 1)
                            dve.wait_ge(fin_var, g + 1)
                        else:
                            ins.then_inc(fin_step, 1)
                            dve.wait_ge(fin_step, g * steps + YS + (n + 1 if n < 5 else n))
                    dve.wait_ge(fin_sq, g + 1)
                    v.reciprocal(lnt[:, 6, r], lnt[:, 5, r]).then_inc(fin_step, 1)
                    dve.wait_ge(fin_step, (g + 1) * steps)
                    v.scalar_tensor_tensor(lnt[:, 7, r], lnt[:, 4, r], -1.0, lnt[:, 6, r], ALU.mult, ALU.mult).then_inc(fin_scale, 1)


def kernel(L0_attn_x, L0_attn_W1, L0_attn_b1, L0_attn_W2, L0_attn_b2, L0_ffn_gate_w, L0_ffn_gate_proj_w,
           L0_ffn_up_proj_w, L0_ffn_down_proj_w):
    import concourse.bacc as bacc
    from concourse.bass_utils import run_bass_kernel_spmd

    x = np.asarray(L0_attn_x)
    turned = [np.asarray(w).reshape(E, H, DC, P).transpose(0, 3, 2, 1).reshape(E, P, DC * H)
              for w in (L0_ffn_gate_proj_w, L0_ffn_up_proj_w)]
    down = np.asarray(L0_ffn_down_proj_w).reshape(E, D, HC, P).transpose(0, 3, 2, 1).reshape(E, P, HC * D)
    arrays = {
        "xT": x.transpose(0, 2, 1),
        "xN": x.reshape(T, D),
        "W1": np.asarray(L0_attn_W1),
        "b1": np.asarray(L0_attn_b1).reshape(DC, P).T,
        "W2": np.asarray(L0_attn_W2).reshape(DC, P, D).transpose(1, 0, 2),
        "b2": np.asarray(L0_attn_b2).reshape(DC, P).T,
        "gateT": np.asarray(L0_ffn_gate_w).reshape(E, DC, P).transpose(2, 1, 0),
        "experts": np.concatenate(turned + [down], axis=2),
    }
    arrays.update(constants())
    arrays = {k: np.ascontiguousarray(v) for k, v in arrays.items()}
    nc = bacc.Bacc("TRN2", target_bir_lowering=False, num_devices=1)
    aps = {k: nc.dram_tensor(f"in_{k}", v.shape, mybir.dt.from_np(v.dtype), kind="ExternalInput").ap() for k, v in arrays.items()}
    out = nc.dram_tensor("out_y", (T, D), F32, kind="ExternalOutput").ap()
    build(nc, out=out, **aps)
    r = run_bass_kernel_spmd(nc, [{f"in_{k}": v for k, v in arrays.items()}], core_ids=[0])
    return r.results[0]["out_y"].reshape(B, L, D)
```

```python
from contextlib import ExitStack

import numpy as np

import concourse.bass as bass
from concourse import mybir

P = 128
B, L, D = 2, 2048, 256
T = B * L
NI = T // P
NB = NI // B
FO = 64
N1, N2 = L // P, P
GD = P // N1
LG = 8
LOADS = D // GD // LG
FILLS = D // GD // 2
CH = 32
NCH = D // CH
E, H, K = 8, 512, 2
CAP = int(1.25 * T / E)
RT = CAP // P
HALF = CAP // 2
ROWS = E * CAP
ZR = 4
YS = 4
GROUPS = ((0, NI // 2), (NI // 2, NI - YS), (NI - YS, NI))
ZEROS = ROWS // P // ZR
DC, HC = D // P, H // P
WPART = DC * H
WSCALE = 16.0
EPS = 1e-5
OUT_OF_RANGE = 32768.0

F32 = mybir.dt.float32
F16 = mybir.dt.float16
U32 = mybir.dt.uint32
ALU = mybir.AluOpType
ACT = mybir.ActivationFunctionType
X = mybir.AxisListType.X


def constants():
    f = np.float32
    c = {}
    pos = np.arange(L, dtype=f)[:, None]
    div = np.exp(np.arange(0, FO, 2, dtype=f) * f(-np.log(f(10000.0)) / f(FO)))
    ang = (pos * div).astype(f)
    pe = np.zeros((L, FO), f)
    pe[:, 0::2] = np.sin(ang)
    pe[:, 1::2] = np.cos(ang)
    c["posT"] = np.ascontiguousarray(pe.T)
    n1 = np.arange(N1)[:, None]
    k1 = np.arange(N1)[None, :]
    th = 2 * np.pi * n1 * (k1 + 0.25) / N1
    across = np.zeros((GD, N1, N1, 2, GD))
    for d in range(GD):
        across[d, :, :, 0, d] = np.cos(th)
        across[d, :, :, 1, d] = -np.sin(th)
    c["across"] = across.reshape(P, 2 * N1 * GD).astype(f)
    n2 = np.arange(N2, dtype=np.float64)
    forward, inverse = np.zeros((N1, P, 3, P)), np.zeros((N1, P, 3, P))
    for k in range(N1):
        ph = 2 * np.pi * np.outer(n2, k + 0.25 + N1 * n2) / L
        forward[k, :, 0] = np.cos(ph)
        forward[k, :, 1] = -np.sin(ph)
        forward[k, :, 2] = np.sin(ph)
        inverse[k, :, 0] = np.cos(ph).T / L
        inverse[k, :, 1] = np.sin(ph).T / L
        inverse[k, :, 2] = -np.sin(ph).T / L
    high = forward.astype(np.float16)
    low = (forward - high).astype(np.float16)
    c["forward"] = np.stack([high, low], axis=3).reshape(N1, P, 6 * P)
    c["inverse"] = inverse.reshape(N1, P, 3 * P).astype(f)
    back = np.zeros((4, N1, 2, 2, N1, 4, 2))
    for q in range(4):
        for h in range(2):
            back[q, :, 0, h, :, q, h] = np.cos(th).T
            back[q, :, 1, h, :, q, h] = -np.sin(th).T
    c["back"] = back.reshape(P, 2 * P).astype(f)
    c["ident"] = np.eye(P, dtype=f)
    c["minus"] = -np.eye(P, dtype=np.float16)
    c["below"] = np.triu(np.ones((P, P)), 1).astype(f)
    rows = np.zeros((P, K * E * NB + E + E + NI))
    mask = np.ones((K * E, NB))
    mask[:, 0] = 0
    rows[:, 0:K * E * NB] = mask.reshape(-1)
    rows[:, K * E * NB:K * E * NB + E] = np.arange(E) * CAP - 1
    rows[:, K * E * NB + E:K * E * NB + 2 * E] = E - np.arange(E)
    col = np.arange(NI)
    rows[:, K * E * NB + 2 * E:] = col // NB * L + NB * np.arange(P)[:, None] + col % NB
    c["rows"] = rows.astype(f)
    return c


def build(nc, xT, W1, b1, W2, b2, gateT, experts, posT, across, forward, inverse, back, ident, minus, below, rows, out):
    fil_dram = nc.dram_tensor("fil_dram", (D, L), F32, kind="Internal").ap()
    xg_dram = [nc.dram_tensor(f"xg{k}_dram", (ROWS, D + 1), F32, kind="Internal").ap() for k in range(K)]
    y_dram = [nc.dram_tensor(f"y{k}_dram", (T, D), F32, kind="Internal").ap() for k in range(K)]

    ctx = ExitStack()
    with ctx:
        def sem(name):
            return ctx.enter_context(nc.semaphore(name))

        def sb(stack, name, shape, dt=F32):
            return stack.enter_context(nc.sbuf_tensor(name, shape, dt))

        xrow = sb(ctx, "xrow", [P, NI, D + 1])
        xn = xrow[:, :, 0:D]
        c_ident = sb(ctx, "c_ident", [P, P])
        c_minus = sb(ctx, "c_minus", [P, P], F16)
        c_below = sb(ctx, "c_below", [P, P])
        c_rows = sb(ctx, "c_rows", [P, K * E * NB + 2 * E + NI])
        c_ones = sb(ctx, "c_ones", [P, P])
        c_gate = sb(ctx, "c_gate", [P, DC, E])
        stats = sb(ctx, "stats", [P, NI, 6])
        lnt = sb(ctx, "lnt", [P, 8, NI])
        w_top = sb(ctx, "w_top", [P, K, NI])
        idx_put = sb(ctx, "idx_put", [P, K, NI], U32)

        conv = ExitStack()
        c_across = sb(conv, "c_across", [P, 2 * N1 * GD])
        c_back = sb(conv, "c_back", [P, 2, P])
        ring = [sb(conv, f"ring{s}", [P, LG, N2]) for s in range(2)]
        over = ExitStack()
        x1f = [sb(over, f"x1f{part}", [P, 2 * N1, D], F16) for part in "hl"]
        over.close()
        bufa = sb(conv, "bufa", [P, 2 * N1 * D])
        x1b = [sb(conv, f"x1b{part}", [P, 2 * N1, D], F16) for part in "hl"]
        matf = [sb(conv, f"matf{s}", [P, 3, 2, P], F16) for s in range(4)]
        mati = [sb(conv, f"mati{s}", [P, 3, P]) for s in range(4)]
        fhat = sb(conv, "fhat", [P, N1, 2, D])
        prod = [sb(conv, f"prod{s}", [P, 2, 2, D]) for s in range(2)]
        yhat = [sb(conv, f"yhat{s}", [P, 2, D]) for s in range(2)]
        zt = [sb(conv, f"zt{s}", [P, CH * 32]) for s in range(2)]
        w1 = sb(conv, "w1", [FO, D])
        w2 = sb(conv, "w2", [P, DC, D])
        bias = sb(conv, "bias", [P, 2, DC])
        zeros = sb(conv, "zeros", [P, ZR, D + 1])
        xts = [sb(conv, f"xts{s}", [P, 2, 2, DC, P], F16) for s in range(3)]
        gs = sb(conv, "gs", [P, DC, E])
        gate16 = sb(conv, "gate16", [P, DC, 2, E], F16)
        rt = sb(conv, "rt", [P, 8, NB * E])
        small = sb(conv, "small", [P, 8, NB])
        oh = sb(conv, "oh", [P, K, E, NB])
        scan = sb(conv, "scan", [P, K, E, NB])
        rk = sb(conv, "rk", [P, K, E, NB])
        red = sb(conv, "red", [P, 6, K, NB])
        tot = sb(conv, "tot", [P, B, K * E])
        gsum = sb(conv, "gsum", [P, E])
        z = bufa.rearrange("p (c k) -> p c k", k=2 * N1)
        fT = bufa[:, 0:DC * L].rearrange("p (c l) -> p c l", c=DC)
        early = fhat.rearrange("p k r d -> p (k r d)")
        hT = early[:, 0:DC * L].rearrange("p (c l) -> p c l", c=DC)
        pos = early[0:FO, DC * L:DC * L + L]
        conv.close()

        moe = ExitStack()
        wh = sb(moe, "wh", [P, E, 3 * WPART], F16)
        wl = sb(moe, "wl", [P, E, 3 * WPART], F16)
        yg = [sb(moe, f"yg{s}", [P, YS, D]) for s in range(2)]
        tok = [sb(moe, f"tok{s}", [P, RT], U32) for s in range(2)]
        tok_y = [sb(moe, f"tok_y{s}", [P, RT], U32) for s in range(2)]
        run = ExitStack()
        wst = [sb(run, f"wst{s}", [P, WPART]) for s in range(2)]
        xg = [sb(run, f"xg{s}", [P, RT, D + 1]) for s in range(2)]
        xth = [sb(run, f"xth{s}", [P, DC, CAP], F16) for s in range(2)]
        xtl = [sb(run, f"xtl{s}", [P, DC, CAP], F16) for s in range(2)]
        ah = [sb(run, f"ah{s}", [P, HC, CAP], F16) for s in range(2)]
        al = [sb(run, f"al{s}", [P, HC, CAP], F16) for s in range(2)]
        s32 = [sb(run, f"s32_{s}", [P, HALF]) for s in range(2)]
        a32 = [sb(run, f"a32_{s}", [P, HALF]) for s in range(2)]
        ysb = [sb(run, f"ysb{s}", [P, RT, D]) for s in range(2)]
        run.close()
        y2 = sb(moe, "y2", [P, NI, D])
        moe.close()

        ps = ctx.enter_context(nc.psum_tensor("ps", [P, 8, 512], F32))

        in_layer1, in_pos, in_layer2, in_across, in_back, in_const = (sem(n) for n in (
            "in_layer1", "in_pos", "in_layer2", "in_across", "in_back", "in_const"))
        in_ring = [sem(f"in_ring{s}") for s in range(2)]
        in_mats = [sem(f"in_mats{s}") for s in range(4)]
        fil_stored = [sem(f"fil_stored{c}") for c in range(DC)]
        zero_stored = sem("zero_stored")
        put_done = [sem(f"put_done{k}") for k in range(K)]
        in_xg = [sem(f"in_xg{s}") for s in range(2)]
        in_w = [sem(f"in_w{s}") for s in range(2)]
        y_zeroed = sem("y_zeroed")
        y_put = [sem(f"y_put{s}") for s in range(2)]
        in_yg = [sem(f"in_yg{s}") for s in range(2)]
        in_y2 = [sem(f"in_y2_{g}") for g in range(NI // YS)]
        out_stored = sem("out_stored")
        h_full, h_done, f_full, f_done, tap_done, zeros_set = (sem(n) for n in ("h_full", "h_done", "f_full", "f_done", "tap_done", "zeros_set"))
        x1h_done = sem("x1h_done")
        x1_full, x1_done = sem("x1_full"), sem("x1_done")
        fwd_full, fhat_done, prod_done, y_ready = (sem(n) for n in ("fwd_full", "fhat_done", "prod_done", "y_ready"))
        z_full, z_done = sem("z_full"), sem("z_done")
        zt_done, back_full, back_kept = sem("zt_done"), sem("back_full"), sem("back_kept")
        st_done, ln_step, sq_done = sem("st_done"), sem("ln_step"), sem("sq_done")
        gate_split, cols_turned, cols_hi, low_left, xts_done, logits_full, normed, gsum_full = (sem(n) for n in (
            "gate_split", "cols_turned", "cols_hi", "low_left", "xts_done", "logits_full", "normed", "gsum_full"))
        r_step, e_ready, e_done, tot_ready, base_full, idx_ready, gate_done = (sem(n) for n in (
            "r_step", "e_ready", "e_done", "tot_ready", "base_full", "idx_ready", "gate_done"))
        xt_full, xth_done, xtl_done = sem("xt_full"), sem("xth_done"), sem("xtl_done")
        wh_done, wl_done = sem("wh_done"), sem("wl_done")
        gu_full, s_done, a_done, ah_done, al_done = (sem(n) for n in ("gu_full", "s_done", "a_done", "ah_done", "al_done"))
        y_full, y_done = sem("y_full"), sem("y_done")
        ids_read, tok_done = sem("ids_read"), sem("tok_done")
        y_room = sem("y_room")
        weighed, pool_sums, dve_sums = sem("weighed"), sem("pool_sums"), sem("dve_sums")
        yg_used = sem("yg_used")
        fin_step, fin_var, fin_sq, fin_scale, fin_done, fin_pool = (sem(n) for n in (
            "fin_step", "fin_var", "fin_sq", "fin_scale", "fin_done", "fin_pool"))

        XT_PER = (RT + 1) // 2
        Q_PER = 2 * HC
        POOL_COLUMNS = [i for i in range(NI) if i % 2]
        TURNED = (4, 5, 7)
        TURNS_AT = {1: (0, 1), 3: (2,)}
        src_x = xT.rearrange("b (s g p) (n m) -> b s (p n) g m", s=LOADS, g=LG, n=N1)
        src_f = fil_dram.rearrange("(s g p) (n m) -> s (p n) g m", s=LOADS, g=LG, n=N1)
        xg_v = [t.rearrange("(n j p) d -> n p j d", j=RT, p=P) for t in xg_dram]
        y_zero = [t.rearrange("(n p r) d -> n p r d", p=P, r=ZR) for t in y_dram]
        y_v = [t.rearrange("(b p i) d -> b p i d", b=B, p=P) for t in y_dram]
        xg_zero = [t.rearrange("(p n r) d -> n p (r d)", p=P, r=ZR) for t in xg_dram]
        out_v = out.rearrange("(b p i) d -> b p i d", b=B, p=P)

        def x1_columns(t, j4, s):
            return t[:, :, bass.ds(8 * GD * j4 + s * 2 * GD, 2 * GD)].rearrange("p k (g d) -> p k g d", g=2)

        block = ctx.enter_context(nc.Block())

        @block.sync
        def _(sp):
            sp.dma_start(w1[:, :], W1).then_inc(in_layer1, 16)
            sp.dma_start(pos[:, 0:512], posT[:, 0:512]).then_inc(in_layer1, 16)
            sp.dma_start(bias[:, 0, :], b1).then_inc(in_layer1, 16)
            sp.dma_start(pos[:, 512:L], posT[:, 512:L]).then_inc(in_pos, 16)
            for dst, src in ((w2[:, :, :], W2), (bias[:, 1, :], b2)):
                sp.dma_start(dst, src).then_inc(in_layer2, 16)
            sp.dma_start(c_across[:, :], across).then_inc(in_across, 16)

            def load_ring(m, l2, s, src):
                sp.wait_ge(x1_full, 4 * (LOADS * m + 2 * l2 + s) + 4)
                sp.dma_start(ring[s][:, :, :], src[2 * l2 + s]).then_inc(in_ring[s], 16)

            def load_mats(s, k, both=True):
                sp.dma_start(matf[s].rearrange("p m h c -> p (m h c)"), forward[k]).then_inc(in_mats[s], 16)
                if both:
                    sp.dma_start(mati[s].rearrange("p m c -> p (m c)"), inverse[k]).then_inc(in_mats[s], 16)

            for l2 in range(LOADS // 2):
                for s in range(2):
                    load_ring(0, l2, s, src_x[0])
            for s in range(4):
                load_mats(s, s, both=False)
            for l2 in range(LOADS // 2):
                sp.wait_ge(fil_stored[l2], 16)
                for s in range(2):
                    load_ring(1, l2, s, src_f)
            with sp.Fori(1, N1 // 4) as k4:
                for s in range(4):
                    sp.wait_ge(fwd_full, 4 * k4 + s - 3)
                    load_mats(s, 4 * k4 + s, both=False)
            for s in range(4):
                sp.wait_ge(fwd_full, N1 + s - 3)
                load_mats(s, s)
            for s in range(2):
                load_ring(2, 0, s, src_x[1])
            with sp.Fori(1, N1 // 4) as k4:
                for s in range(4):
                    sp.wait_ge(z_full, 4 * k4 + s - 3)
                    load_mats(s, 4 * k4 + s)
            for s in range(2):
                load_ring(2, 1, s, src_x[1])
            with sp.Fori(0, N1 // 4) as k4:
                for s in range(4):
                    sp.wait_ge(z_full, N1 + 4 * k4 + s - 3)
                    load_mats(s, 4 * k4 + s)

            def load_rows(s, k, e):
                n = k * E + e
                if not (isinstance(n, int) and n < 2):
                    sp.wait_ge(ids_read, n - 1)
                sp.dma_start(xg[s][:, :, :], xg_v[k][e]).then_inc(in_xg[s], 16)

            def load_weights(e, parity):
                for j in range(3):
                    s = (3 * parity + j) % 2
                    sp.wait_ge(wl_done, 3 * e + j + 1)
                    sp.dma_start(wst[s][:, :], experts[e, :, j * WPART:(j + 1) * WPART]).then_inc(in_w[s], 16)

            def load_first(half, s):
                g = 2 * half + s
                sp.wait_ge(yg_used, YS * g + YS)
                b, i = YS * g // NB, YS * g % NB
                sp.dma_start(yg[s][:, :, :], y_v[0][b, :, i:i + YS, :]).then_inc(in_yg[s], 16)

            sp.wait_ge(gate_done, 1)
            load_weights(0, 0)
            sp.wait_ge(put_done[0], 16 * NI)
            load_rows(0, 0, 0)
            load_rows(1, 0, 1)
            load_rows(0, 0, 2)
            load_weights(1, 1)
            with sp.Fori(0, (E - 4) // 2) as e2:
                e = 2 * e2 + 1
                for s in (1, 0):
                    load_rows(s, 0, e + (1 - s) + 2)
                    load_weights(e + (1 - s) + 1, 1 - s)
            load_rows(1, 0, E - 1)
            load_weights(E - 2, 0)
            sp.wait_ge(put_done[1], 16 * NI)
            load_rows(0, 1, 0)
            load_weights(E - 1, 1)
            load_rows(1, 1, 1)
            load_rows(0, 1, 2)
            for s in range(2):
                sp.wait_ge(y_put[s], 16 * RT * (E // 2))
            load_first(0, 0)
            for e in range(1, E - 2):
                load_rows(e % 2, 1, e + 2)
                load_first(e // 2, e % 2)
            for g in range(E - 2, NI // YS):
                load_first(g // 2, g % 2)
            for s in range(2):
                sp.wait_ge(y_put[s], 16 * RT * (E // 2) * K)
            for g in range(NI // YS):
                b, i = YS * g // NB, YS * g % NB
                sp.dma_start(y2[:, YS * g:YS * (g + 1), :], y_v[1][b, :, i:i + YS, :]).then_inc(in_y2[g], 16)
            for g in range(NI // YS):
                sp.wait_ge(fin_done, (YS - 1) * (g + 1))
                sp.wait_ge(fin_pool, g + 1)
                b, i = YS * g // NB, YS * g % NB
                sp.dma_start(out_v[b, :, i:i + YS, :], xn[:, YS * g:YS * (g + 1), :]).then_inc(out_stored, 16)
            sp.wait_ge(out_stored, 16 * (NI // YS))

        @block.gpsimd
        def _(pool):
            nc.gpsimd.memset(zeros[:, :, 0:D], 0.0).then_inc(zeros_set, 1)
            nc.gpsimd.memset(zeros[:, :, D:D + 1], OUT_OF_RANGE).then_inc(zeros_set, 1)
            nc.gpsimd.memset(c_ones[:, :], 1.0).then_inc(zeros_set, 1)
            pool.wait_ge(zeros_set, 3)
            for k, (paced_by, begin) in enumerate(((h_full, 1), (x1_full, 8 + FILLS + FILLS // 2))):
                with pool.Fori(0, T // P // ZR) as n:
                    pool.wait_ge(paced_by, n + begin)
                    pool.dma_start(y_zero[k][n], zeros[:, :, 0:D]).then_inc(y_zeroed, 16)
            for k in range(K):
                with pool.Fori(0, ZEROS) as n:
                    pool.wait_ge(fwd_full, N1 + ZEROS * k + n + 2)
                    pool.dma_start(xg_zero[k][n], zeros.rearrange("p r d -> p (r d)")).then_inc(zero_stored, 16)
            pool.wait_ge(zero_stored, 16 * K * ZEROS)
            for b in range(B):
                pool.wait_ge(idx_ready, b + 1)
                for k in range(K):
                    for i in range(b * NB, (b + 1) * NB):
                        if k == 0:
                            pool.wait_ge(normed, i + 1)
                        nc.gpsimd.indirect_dma_start(
                            xg_dram[k][:, :], bass.IndirectOffsetOnAxis(ap=idx_put[:, k, i:i + 1], axis=0), xrow[:, i, :], None,
                            bounds_check=ROWS - 1, oob_is_err=False).then_inc(put_done[k], 16)
            pool.wait_ge(y_zeroed, 16 * K * (T // P // ZR))
            for n in range(K * E):
                pool.wait_ge(tok_done, n + 1)
                for t in range(RT):
                    pool.wait_ge(y_done, 2 + RT * n + t + 1)
                    nc.gpsimd.indirect_dma_start(
                        y_dram[n // E][:, :], bass.IndirectOffsetOnAxis(ap=tok_y[n % 2][:, t:t + 1], axis=0), ysb[n % 2][:, t, :], None,
                        bounds_check=T - 1, oob_is_err=False).then_inc(y_put[n % 2], 16)
                if n:
                    pool.wait_ge(y_put[(n - 1) % 2], 16 * RT * ((n - 1) // 2 + 1))
                    pool.sem_inc(y_room, 1)
            pool.wait_ge(yg_used, 2 * YS + NI)
            for i in POOL_COLUMNS:
                pool.wait_ge(weighed, POOL_COLUMNS.index(i) + 1)
                nc.gpsimd.tensor_tensor(y2[:, i, :], y2[:, i, :], xn[:, i, :], ALU.add).then_inc(pool_sums, 1)
            for g, (lo, hi) in enumerate(GROUPS):
                pool.wait_ge(fin_scale, g + 1)
                for i in range(lo + YS - 1, hi, YS):
                    nc.gpsimd.tensor_scalar(xn[:, i, :], y2[:, i, :], lnt[:, 6, i:i + 1], lnt[:, 7, i:i + 1], ALU.mult, ALU.add).then_inc(fin_pool, 1)

        @block.scalar
        def _(act):
            act.sem_inc(z_done, 4)
            act.sem_inc(back_kept, 2)
            act.sem_inc(y_done, 2)
            act.sem_inc(fhat_done, 2)
            act.sem_inc(y_room, 2)
            act.wait_ge(in_layer1, 48)
            for n in range(DC * 4):
                act.wait_ge(h_full, n + 1)
                nc.scalar.activation(hT[:, n // 4, (n % 4) * 512:(n % 4 + 1) * 512], ps[:, n % 4, :], ACT.Gelu,
                                     bias=bias[:, 0, n // 4:n // 4 + 1]).then_inc(h_done, 1)
            act.wait_ge(in_layer2, 32)
            for n in range(DC * 4):
                act.wait_ge(f_full, n + 1)
                nc.scalar.activation(fT[:, n // 4, (n % 4) * 512:(n % 4 + 1) * 512], ps[:, 4 + n % 4, :], ACT.Identity,
                                     bias=bias[:, 1, n // 4:n // 4 + 1]).then_inc(f_done, 1)
                if n % 4 == 3:
                    act.wait_ge(f_done, n + 1)
                    act.wait_ge(tap_done, n // 4 + 1)
                    act.dma_start(fil_dram[(n // 4) * P:(n // 4 + 1) * P, :], fT[:, n // 4, :]).then_inc(fil_stored[n // 4], 16)

            act.dma_start(c_back[:, :, :], back.rearrange("p (h m) -> p h m", h=2)).then_inc(in_back, 16)
            for dst, src in ((c_ident[:, :], ident), (c_minus[:, :], minus), (c_below[:, :], below), (c_rows[:, :], rows), (c_gate[:, :, :], gateT)):
                act.dma_start(dst, src).then_inc(in_const, 16)

            def keep_x1(m, buf):
                with act.Fori(0, FILLS // 4) as j4:
                    for s in range(4):
                        act.wait_ge(x1_full, 8 + FILLS * m + 4 * j4 + s + 1)
                        nc.scalar.activation(x1_columns(buf[0], j4, s), ps[:, s, :].rearrange("p (g k d) -> p k g d", g=2, d=GD),
                                             ACT.Copy).then_inc(x1h_done, 1)

            zv = z.rearrange("p c k -> p k c")

            def keep_z(b, k, s):
                act.wait_ge(z_full, b * N1 + k + 1)
                nc.scalar.activation(zv[:, bass.ds(2 * k, 2), :], ps[:, 4 + s, :].rearrange("p (r c) -> p r c", r=2),
                                     ACT.Copy).then_inc(z_done, 1)

            def keep_back(b):
                with act.Fori(0, NCH // 2) as c2:
                    for s in range(2):
                        act.wait_ge(back_full, NCH * b + 2 * c2 + s + 1)
                        nc.scalar.activation(xn[:, b * NB:(b + 1) * NB, bass.ds((2 * c2 + s) * CH, CH)],
                                             ps[:, 6 + s, :].rearrange("p (d i) -> p i d", i=NB), ACT.Copy).then_inc(back_kept, 1)

            def deviation(b):
                act.wait_ge(ln_step, 9 * b + 6)
                nc.scalar.activation(lnt[:, 5, b * NB:(b + 1) * NB], lnt[:, 3, b * NB:(b + 1) * NB], ACT.Sqrt).then_inc(sq_done, 1)

            def keep_turned(b):
                for q in range(NB // 2 + 1):
                    n = b * (NB // 2) + q
                    if q < NB // 2:
                        act.wait_ge(cols_turned, n + 1)
                        if n >= 3:
                            act.wait_ge(logits_full, n - 2)
                        nc.scalar.activation(xts[q % 3][:, 0].rearrange("p t c r -> p (t c r)"), ps[:, TURNED[q % 3], :], ACT.Copy).then_inc(cols_hi, 1)
                    if q == NB // 2 - 1:
                        deviation(b)
                    if q:
                        act.wait_ge(low_left, n)
                        nc.scalar.activation(xts[(q - 1) % 3][:, 1].rearrange("p t c r -> p (t c r)"), ps[:, TURNED[(q - 1) % 3], :], ACT.Copy).then_inc(xts_done, 1)

            def normalise(lo, hi):
                for i in range(lo, hi):
                    nc.scalar.activation(xn[:, i, :], xn[:, i, :], ACT.Identity, bias=lnt[:, 7, i:i + 1], scale=lnt[:, 6, i:i + 1]).then_inc(normed, 1)

            def exps(b):
                act.wait_ge(e_ready, b + 1)
                act.wait_ge(cols_turned, NB // 2 * (b + 1))
                nc.scalar.activation(rt[:, 2, :], rt[:, 1, :], ACT.Exp).then_inc(e_done, 1)

            keep_x1(0, x1b)
            for c in range(DC):
                act.wait_ge(fil_stored[c], 16)
            keep_x1(1, x1f)
            with act.Fori(0, N1 // 2) as k2:
                for s in range(2):
                    k = 2 * k2 + s
                    act.wait_ge(fwd_full, k + 1)
                    nc.scalar.activation(fhat[:, bass.ds(k, 1), :, :].rearrange("p a r d -> p (a r d)"), ps[:, s, :],
                                         ACT.Copy).then_inc(fhat_done, 1)
            with act.Fori(0, N1 // 2) as k2:
                for s in range(2):
                    keep_z(0, 2 * k2 + s, s)
            keep_back(0)
            keep_x1(2, x1b)
            keep_turned(0)
            exps(0)
            for k in range(4):
                keep_z(1, k, k % 2)
                normalise(k * NB // 4, (k + 1) * NB // 4)
            with act.Fori(2, N1 // 2) as k2:
                for s in range(2):
                    keep_z(1, 2 * k2 + s, s)
            keep_back(1)
            keep_turned(1)
            exps(1)
            normalise(NB, 2 * NB)

            def turn_hi(n, s, j):
                w = 2 if 2 * j + 1 < RT else 1
                act.wait_ge(xt_full, 2 * XT_PER + XT_PER * n + j + 1)
                nc.scalar.activation(
                    xth[s][:, :, 2 * j * P:(2 * j + w) * P].rearrange("p c (t r) -> p t c r", t=w),
                    ps[:, 4 + j % 2, 0:w * D].rearrange("p (t c r) -> p t c r", t=w, c=DC), ACT.Copy).then_inc(xth_done, 1)

            def weights_hi(e, parity, j):
                s = (3 * parity + j) % 2
                act.wait_ge(in_w[s], 24 * (e - parity) + 16 * ((3 * parity + j) // 2 + 1))
                nc.scalar.activation(wh[:, bass.ds(e, 1), j * WPART:(j + 1) * WPART],
                                     wst[s][:, :].unsqueeze(1), ACT.Copy, scale=WSCALE).then_inc(wh_done, 1)

            def a_hi(n, s, j):
                act.wait_ge(a_done, 2 + Q_PER * n + j + 1)
                nc.scalar.activation(ah[s][:, j // 2, (j % 2) * HALF:(j % 2 + 1) * HALF], a32[j % 2][:, :],
                                     ACT.Copy).then_inc(ah_done, 1)

            def keep_y(n, s, t):
                if t == 0:
                    act.wait_ge(y_room, n + 1)
                act.wait_ge(y_full, RT * n + t + 1)
                nc.scalar.activation(ysb[s][:, t, :], ps[:, 6 + (RT * s + t) % 2, 0:D], ACT.Copy, scale=1.0 / WSCALE).then_inc(y_done, 1)

            def expert(n, s, split=False, turn=True, last_rows=True):
                for j in range(Q_PER):
                    act.wait_ge(gu_full, Q_PER * n + j + 1)
                    act.wait_ge(a_done, Q_PER * n + j + 1)
                    nc.scalar.activation(s32[j % 2][:, :], ps[:, 2 * (j % 2), 0:HALF], ACT.Silu, scale=1.0 / WSCALE).then_inc(s_done, 1)
                    if j:
                        a_hi(n, s, j - 1)
                    if turn and j in TURNS_AT:
                        for t in TURNS_AT[j]:
                            turn_hi(n + 1, 1 - s, t)
                    if last_rows and 2 <= j < 2 + RT - (not turn):
                        keep_y(n - 1, 1 - s, j - 2)
                    if split and j in (2, 4, 6):
                        weights_hi(n + 1, 1 - s, j // 2 - 1)
                a_hi(n, s, Q_PER - 1)
                if not turn:
                    keep_y(n - 1, 1 - s, RT - 1)

            for j in range(3):
                weights_hi(0, 0, j)
            for j in range(XT_PER):
                turn_hi(0, 0, j)
            expert(0, 0, split=True, last_rows=False)
            with act.Fori(0, (E - 2) // 2) as n2:
                n = 2 * n2 + 1
                expert(n, 1, split=True)
                expert(n + 1, 0, split=True)
            expert(E - 1, 1)
            expert(E, 0)
            with act.Fori(0, (E - 2) // 2) as n2:
                n = 2 * n2 + E + 1
                expert(n, 1)
                expert(n + 1, 0)
            expert(2 * E - 1, 1, turn=False)
            for t in range(RT):
                keep_y(2 * E - 1, 1, t)
            for i in POOL_COLUMNS:
                act.wait_ge(in_y2[i // YS], 16)
                nc.scalar.activation(y2[:, i, :], y2[:, i, :], ACT.Copy, scale=w_top[:, 1, i:i + 1]).then_inc(weighed, 1)

            def last_deviation(g):
                lo, hi = GROUPS[g]
                act.wait_ge(fin_var, g + 1)
                nc.scalar.activation(lnt[:, 5, lo:hi], lnt[:, 3, lo:hi], ACT.Sqrt).then_inc(fin_sq, 1)

            last_deviation(0)
            for g, (lo, hi) in enumerate(GROUPS):
                act.wait_ge(fin_scale, g + 1)
                for i in range(lo, hi):
                    if i == hi - YS // 2 and g + 1 < len(GROUPS):
                        last_deviation(g + 1)
                    if i % YS < YS - 1:
                        nc.scalar.activation(xn[:, i, :], y2[:, i, :], ACT.Identity, bias=lnt[:, 7, i:i + 1], scale=lnt[:, 6, i:i + 1]).then_inc(fin_done, 1)

        @block.tensor
        def _(pe):
            pe.sem_inc(x1_full, 8)
            pe.sem_inc(xt_full, 2 * XT_PER)
            mm = nc.tensor.matmul
            pe.wait_ge(in_layer1, 48)
            for n in range(DC * 4):
                if n == 1:
                    pe.wait_ge(in_pos, 16)
                if n >= 4:
                    pe.wait_ge(h_done, n - 3)
                mm(ps[:, n % 4, :], w1[:, (n // 4) * P:(n // 4 + 1) * P], pos[:, (n % 4) * 512:(n % 4 + 1) * 512],
                   start=True, stop=True).then_inc(h_full, 1)
            pe.wait_ge(in_layer2, 32)
            for n in range(DC * 4):
                pe.wait_ge(h_done, DC * 4)
                if n >= 4:
                    pe.wait_ge(f_done, n - 3)
                for c in range(DC):
                    last = mm(ps[:, 4 + n % 4, :], w2[:, c, (n // 4) * P:(n // 4 + 1) * P],
                              hT[:, c, (n % 4) * 512:(n % 4 + 1) * 512], start=(c == 0), stop=(c == DC - 1))
                last.then_inc(f_full, 1)

            def go_across(m):
                with pe.Fori(0, LOADS // 2) as l2:
                    for s in range(2):
                        pe.wait_ge(in_ring[s], 16 * (LOADS // 2 * m + l2 + 1))
                        for j in range(4):
                            pe.wait_ge(x1_done, FILLS * m + 8 * l2 + 4 * s + j + 1)
                            for g in range(2):
                                last = mm(ps[:, j, g * 256:(g + 1) * 256], ring[s][:, 2 * j + g, :], c_across[:, :],
                                          start=True, stop=True)
                            last.then_inc(x1_full, 1)

            def forward(m, k, buf, s, ms):
                if isinstance(m, int) and m == 0:
                    pe.wait_ge(in_mats[ms], 4 * (k - ms) + 16)
                else:
                    pe.wait_ge(in_mats[ms], 4 * N1 + 8 * (N1 * (m - 1) + k - ms) + 32)
                (reh, imh), (rel, iml) = ([t[:, bass.ds(2 * k + j, 1), :].rearrange("p a c -> p (a c)") for j in range(2)] for t in buf)

                def product(o, terms):
                    for n, (j, xhi, xlo) in enumerate(terms):
                        whi, wlo = matf[ms][:, j, 0, :], matf[ms][:, j, 1, :]
                        mm(o, whi, xhi, start=(n == 0), stop=False)
                        mm(o, whi, xlo, start=False, stop=False)
                        last = mm(o, wlo, xhi, start=False, stop=(n == 1))
                    return last

                product(ps[:, s, 0:D], ((0, reh, rel), (2, imh, iml)))
                product(ps[:, s, D:2 * D], ((1, reh, rel), (0, imh, iml))).then_inc(fwd_full, 1)

            def forward_x(b, k, s, ms):
                pe.wait_ge(prod_done, 2 * (N1 * b + k) + 2)
                forward(1 + b, k, x1b, s, ms)

            def inverse(b, k, s, ms):
                n = N1 * b + k
                pe.wait_ge(y_ready, 4 + 2 * n + 2)
                pe.wait_ge(z_done, n + 3)
                w = mati[ms]
                mm(ps[:, 4 + s, 0:D], w[:, 0, :], yhat[s][:, 0, :], start=True, stop=False)
                mm(ps[:, 4 + s, 0:D], w[:, 2, :], yhat[s][:, 1, :], start=False, stop=True)
                mm(ps[:, 4 + s, D:2 * D], w[:, 1, :], yhat[s][:, 0, :], start=True, stop=False)
                mm(ps[:, 4 + s, D:2 * D], w[:, 0, :], yhat[s][:, 1, :], start=False, stop=True).then_inc(z_full, 1)

            def go_back(b):
                with pe.Fori(0, NCH // 2) as c2:
                    for s in range(2):
                        pe.wait_ge(zt_done, NCH * b + 2 * c2 + s + 1)
                        pe.wait_ge(back_kept, NCH * b + 2 * c2 + s + 1)
                        zs = zt[s].rearrange("p (d h i) -> p h d i", h=2, i=NB)
                        for h in range(2):
                            last = mm(ps[:, 6 + s, :], c_back[:, h, :], zs[:, h], start=(h == 0), stop=(h == 1))
                        last.then_inc(back_full, 1)

            def logits(b):
                pe.wait_ge(back_kept, 2 + NCH * (b + 1))
                both = ps[:, 6, 0:2 * NB * E].rearrange("p (h i e) -> p i h e", h=2, e=E)
                for q in range(NB // 2 + 2):
                    n = b * (NB // 2) + q
                    if q < NB // 2:
                        if n >= 3:
                            pe.wait_ge(xts_done, n - 2)
                        for s in range(2):
                            for c in range(DC):
                                o = s * D + c * P
                                last = mm(ps[:, TURNED[q % 3], o:o + P], xn[:, b * NB + 2 * q + s, c * P:(c + 1) * P], c_ident[:, :],
                                          start=(o == 0), stop=False, is_transpose=True, skip_group_check=True)
                        last.then_inc(cols_turned, 1)
                    if 1 <= q <= NB // 2:
                        pe.wait_ge(cols_hi, n)
                        mm(ps[:, TURNED[(q - 1) % 3], :], c_minus[:, :], xts[(q - 1) % 3][:, 0].rearrange("p t c r -> p (t c r)"),
                           start=False, stop=True, skip_group_check=True).then_inc(low_left, 1)
                    if q >= 2:
                        pe.wait_ge(xts_done, n - 1)
                        for s in range(2):
                            i = 2 * (q - 2) + s
                            for c in range(DC):
                                xs = xts[(q - 2) % 3]
                                mm(both[:, i], xs[:, 0, s, c, :], gate16[:, c], start=(c == 0), stop=False, skip_group_check=True)
                                last = mm(both[:, i, 0], xs[:, 1, s, c, :], gate16[:, c, 0], start=False, stop=(c == DC - 1), skip_group_check=True)
                        last.then_inc(logits_full, 1)

            def ranks_base(b):
                pe.wait_ge(tot_ready, b + 1)
                last = mm(ps[:, 6, 2 * P:2 * P + K * E], c_below[:, :], tot[:, b, :], start=True, stop=(b == 0), skip_group_check=True)
                if b:
                    last = mm(ps[:, 6, 2 * P:2 * P + K * E], c_ones[:, :], tot[:, 0, :], start=False, stop=True, skip_group_check=True)
                last.then_inc(base_full, 1)

            pe.wait_ge(in_across, 16)
            go_across(0)
            go_across(1)
            pe.wait_ge(x1_done, 4 + 2 * FILLS)
            with pe.Fori(0, N1 // 4) as k4:
                for s in range(4):
                    pe.wait_ge(fhat_done, 4 * k4 + s + 1)
                    forward(0, 4 * k4 + s, x1f, s % 2, s)
            pe.wait_ge(fhat_done, 2 + N1)
            pe.wait_ge(in_back, 16)
            for b in range(B):
                pe.wait_ge(x1_done, 4 + (2 + b) * FILLS)
                forward_x(b, 0, 0, 0)
                for lo, hi in ((0, 2), (2, N1 // 4 - 1)):
                    with pe.Fori(lo, hi) as k4:
                        for j in range(4):
                            forward_x(b, 4 * k4 + j + 1, (j + 1) % 2, (j + 1) % 4)
                            inverse(b, 4 * k4 + j, j % 2, j)
                    if b == 1 and lo == 0:
                        ranks_base(0)
                for k in range(N1 - 4, N1):
                    if k + 1 < N1:
                        forward_x(b, k + 1, (k + 1) % 2, (k + 1) % 4)
                    inverse(b, k, k % 2, k % 4)
                go_back(b)
                if b == 0:
                    go_across(2)
                    pe.wait_ge(in_const, 80)
                    pe.wait_ge(zeros_set, 3)
                    pe.wait_ge(gate_split, 1)
                    logits(0)
                    for c in range(DC):
                        last = mm(ps[:, 6, 3 * P:3 * P + E], c_ones[:, :], c_gate[:, c, :], start=(c == 0), stop=(c == DC - 1), skip_group_check=True)
                    last.then_inc(gsum_full, 1)
                else:
                    logits(1)
                    ranks_base(1)

            def turn(n, s, j):
                if j == 0:
                    pe.wait_ge(in_xg[s], 8 * (n - s) + 16)
                if j == 2:
                    pe.wait_ge(xtl_done, XT_PER * n + 1)
                for t in range(2 * j, min(2 * j + 2, RT)):
                    for c in range(DC):
                        o = (t % 2) * D + c * P
                        last = nc.tensor.transpose(ps[:, 4 + j % 2, o:o + P], xg[s][:, t, c * P:(c + 1) * P], c_ident[:, :])
                last.then_inc(xt_full, 1)

            def split_mm(o, whi, wlo, xhi, xlo, start, stop):
                mm(o, whi, xhi, start=start, stop=False)
                mm(o, whi, xlo, start=False, stop=False)
                return mm(o, wlo, xhi, start=False, stop=stop)

            def wslice(w, e, off, width):
                return w[:, bass.ds(e, 1), off:off + width].rearrange("p a c -> p (a c)")

            def down(n, e, s, t):
                pe.wait_ge(y_done, RT * n + t + 1)
                if t == 0:
                    pe.wait_ge(al_done, 2 + Q_PER * (n + 1))
                    pe.wait_ge(wl_done, 2 + 3 * (e + 1))
                for c in range(HC):
                    off = 2 * WPART + c * D
                    last = split_mm(ps[:, 6 + (RT * s + t) % 2, 0:D], ah[s][:, c, t * P:(t + 1) * P], al[s][:, c, t * P:(t + 1) * P],
                                    wslice(wh, e, off, D), wslice(wl, e, off, D), c == 0, c == HC - 1)
                last.then_inc(y_full, 1)

            def expert(n, e, s, turn_next=True, last_rows=True, last_e=None, tiles_after=range(1, 1 + RT)):
                pe.wait_ge(xtl_done, XT_PER * (n + 1))
                pe.wait_ge(wl_done, 2 + 3 * e + 2)
                for j in range(Q_PER):
                    pe.wait_ge(a_done, Q_PER * n + j + 1)
                    r = slice((j % 2) * HALF, (j % 2 + 1) * HALF)
                    for part in range(2):
                        for c in range(DC):
                            off = part * WPART + c * H + (j // 2) * P
                            last = split_mm(ps[:, 2 * (j % 2) + part, 0:HALF], wslice(wh, e, off, P), wslice(wl, e, off, P),
                                            xth[s][:, c, r], xtl[s][:, c, r], c == 0, c == DC - 1)
                    last.then_inc(gu_full, 1)
                    if turn_next:
                        for t in TURNS_AT.get(j + 1, ()):
                            turn(n + 1, 1 - s, t)
                    if last_rows and j in tiles_after:
                        down(n - 1, e - 1 if last_e is None else last_e, 1 - s, tiles_after.index(j))

            for j in range(XT_PER):
                turn(0, 0, j)
            expert(0, 0, 0, last_rows=False)
            with pe.Fori(0, (E - 2) // 2) as e2:
                e = 2 * e2 + 1
                expert(e, e, 1)
                expert(e + 1, e + 1, 0)
            expert(E - 1, E - 1, 1)
            expert(E, 0, 0, last_e=E - 1)
            with pe.Fori(0, (E - 2) // 2) as e2:
                e = 2 * e2 + 1
                expert(E + e, e, 1)
                expert(E + e + 1, e + 1, 0)
            expert(2 * E - 1, E - 1, 1, turn_next=False, tiles_after=(1, 2, 3, 4, Q_PER - 1))
            for t in range(RT):
                down(2 * E - 1, E - 1, 1, t)

        @block.vector
        def _(dve):
            v = nc.vector
            dve.sem_inc(x1_done, 4)
            dve.sem_inc(prod_done, 4)
            dve.sem_inc(wl_done, 2)
            dve.sem_inc(a_done, 2)
            dve.sem_inc(yg_used, 2 * YS)
            dve.sem_inc(y_ready, 4)
            dve.sem_inc(al_done, 2)

            def keep_x1(m, buf):
                with dve.Fori(0, FILLS // 4) as j4:
                    for s in range(4):
                        dve.wait_ge(x1h_done, FILLS * m + 4 * j4 + s + 1)
                        v.tensor_tensor(x1_columns(buf[1], j4, s), ps[:, s, :].rearrange("p (g k d) -> p k g d", g=2, d=GD),
                                        x1_columns(buf[0], j4, s), ALU.subtract).then_inc(x1_done, 1)

            def multiply(b, k, s):
                n = N1 * b + k
                dve.wait_ge(fwd_full, N1 + n + 1)
                dve.wait_ge(y_ready, 2 * n + 2)
                xs = ps[:, s, :].rearrange("p (r d) -> p r d", r=2)
                fs = fhat[:, bass.ds(k, 1), :, :].rearrange("p a r d -> p (a r) d")
                v.tensor_tensor(prod[s][:, 0], xs, fs, ALU.mult).then_inc(prod_done, 1)
                v.tensor_tensor(prod[s][:, 1], xs[:, ::-1, :], fs, ALU.mult).then_inc(prod_done, 1)
                dve.wait_ge(prod_done, 2 * n + 6)
                dve.wait_ge(z_done, n + 3)
                for w, op in ((0, ALU.subtract), (1, ALU.add)):
                    v.tensor_tensor(yhat[s][:, w, :], prod[s][:, w, 0], prod[s][:, w, 1], op).then_inc(y_ready, 1)

            def turn_back(b):
                dve.wait_ge(z_done, 4 + N1 * (b + 1))
                for c in range(NCH):
                    n = NCH * b + c
                    if n >= 2:
                        dve.wait_ge(back_full, n - 1)
                    v.transpose(zt[c % 2][:, :], z[:, c * CH:(c + 1) * CH, :].rearrange("p c k -> p (c k)")).then_inc(zt_done, 1)

            def norm_steps(st, lo, hi):
                r = lambda n: lnt[:, n, lo:hi]
                return [
                    lambda: v.tensor_tensor(r(0), st[:, :, 1], st[:, :, 4], ALU.add),
                    lambda: v.tensor_tensor(r(1), st[:, :, 1], st[:, :, 4], ALU.subtract),
                    lambda: v.tensor_tensor(r(2), st[:, :, 2], st[:, :, 5], ALU.add),
                    lambda: v.tensor_tensor(r(1), r(1), r(1), ALU.mult),
                    lambda: v.scalar_tensor_tensor(r(3), r(1), D / 4.0, r(2), ALU.mult, ALU.add),
                    lambda: v.tensor_scalar(r(3), r(3), 1.0 / D, EPS, ALU.mult, ALU.add),
                    lambda: v.tensor_scalar(r(4), r(0), 0.5, None, ALU.mult),
                ]

            def moments(b):
                lo, hi = b * NB, (b + 1) * NB
                dve.wait_ge(back_kept, 2 + NCH * (b + 1))
                for i in range(lo, hi):
                    v.bn_stats(stats[:, i, :], xn[:, i, :]).then_inc(st_done, 1)
                dve.wait_ge(st_done, hi)
                for n, step in enumerate(norm_steps(stats[:, lo:hi], lo, hi)):
                    if n:
                        dve.wait_ge(ln_step, 9 * b + n)
                    step().then_inc(ln_step, 1)
                dve.wait_ge(sq_done, b + 1)
                v.reciprocal(lnt[:, 6, lo:hi], lnt[:, 5, lo:hi]).then_inc(ln_step, 1)
                dve.wait_ge(ln_step, 9 * b + 8)
                v.scalar_tensor_tensor(lnt[:, 7, lo:hi], lnt[:, 4, lo:hi], -1.0, lnt[:, 6, lo:hi], ALU.mult, ALU.mult).then_inc(ln_step, 1)

            count = [0]

            def step(ins):
                ins.then_inc(r_step, 1)
                count[0] += 1
                dve.wait_ge(r_step, count[0])

            def ie(k):
                return rt[:, k, :].rearrange("p (i e) -> p i e", e=E)

            def over_e(ap):
                return ap.unsqueeze(2).to_broadcast([P, NB, E])

            def flat(t):
                return t.rearrange("p k e i -> p (k e i)")

            KEI = K * E * NB
            first_of = c_rows[:, KEI + E:KEI + 2 * E].unsqueeze(1).to_broadcast([P, NB, E])
            region = c_rows[:, KEI:KEI + E].unsqueeze(1).unsqueeze(3).to_broadcast([P, K, E, NB])

            def scores(b):
                mean, scale = (over_e(lnt[:, n, b * NB:(b + 1) * NB]) for n in (4, 6))
                if b == 0:
                    dve.wait_ge(gsum_full, 1)
                    step(v.tensor_copy(gsum[:, :], ps[:, 6, 3 * P:3 * P + E]))
                step(v.tensor_tensor(ie(7), mean, gsum[:, :].unsqueeze(1).to_broadcast([P, NB, E]), ALU.mult))
                dve.wait_ge(logits_full, NB // 2 * (b + 1))
                step(v.scalar_tensor_tensor(rt[:, 5, :], ps[:, 6, 0:NB * E], 1.0 / WSCALE, rt[:, 7, :], ALU.mult, ALU.subtract))
                step(v.scalar_tensor_tensor(rt[:, 0, :], ps[:, 6, NB * E:2 * NB * E], 1.0 / WSCALE, rt[:, 5, :], ALU.mult, ALU.add))
                step(v.tensor_tensor(ie(0), ie(0), scale, ALU.mult))
                step(v.tensor_reduce(small[:, 0, :], ie(0), X, ALU.max))
                v.tensor_tensor(ie(1), ie(0), over_e(small[:, 0, :]), ALU.subtract).then_inc(e_ready, 1)
                dve.wait_ge(e_done, b + 1)

            def pick(b, k):
                e_k, top = ie((2, 4)[k]), small[:, 3 + k, :]
                step(v.tensor_reduce(top, e_k, X, ALU.max))
                step(v.tensor_tensor(ie(5), e_k, over_e(top), ALU.is_equal))
                step(v.tensor_tensor(ie(6), ie(5), first_of, ALU.mult))
                step(v.tensor_reduce(small[:, 5, :], ie(6), X, ALU.max))
                step(v.tensor_tensor(oh[:, k].rearrange("p e i -> p i e"), first_of, over_e(small[:, 5, :]), ALU.is_equal))
                if k == 0:
                    step(v.scalar_tensor_tensor(ie(4), oh[:, 0].rearrange("p e i -> p i e"), -2.0, ie(2), ALU.mult, ALU.add))

            def count_up(b):
                step(v.tensor_tensor_scan(flat(scan), c_rows[:, 0:KEI], flat(oh), 0.0, ALU.mult, ALU.add))
                v.tensor_copy(tot[:, b, :], scan[:, :, :, NB - 1].rearrange("p k e -> p (k e)")).then_inc(tot_ready, 1)
                step(v.tensor_tensor(rk[:, :], region, oh[:, :], ALU.mult))
                step(v.tensor_reduce(red[:, 1], rk[:, :].rearrange("p k e i -> p k i e"), X, ALU.add))

            def place(b):
                dve.wait_ge(base_full, b + 1)
                step(v.tensor_tensor(rk[:, :], scan[:, :], ps[:, 6, 2 * P:2 * P + K * E].rearrange("p (k e) -> p k e", k=K).unsqueeze(3).to_broadcast([P, K, E, NB]), ALU.add))
                step(v.tensor_tensor(rk[:, :], rk[:, :], oh[:, :], ALU.mult))
                step(v.tensor_reduce(red[:, 0], rk[:, :].rearrange("p k e i -> p k i e"), X, ALU.add))
                step(v.tensor_scalar(red[:, 2], red[:, 0], float(CAP), OUT_OF_RANGE, ALU.is_gt, ALU.mult))
                step(v.tensor_tensor(red[:, 3], red[:, 0], red[:, 1], ALU.add))
                v.tensor_tensor(idx_put[:, :, b * NB:(b + 1) * NB], red[:, 3], red[:, 2], ALU.add).then_inc(idx_ready, 1)

            def probabilities():
                step(v.tensor_scalar(red[:, 5], red[:, 0], float(CAP), None, ALU.is_le))
                step(v.tensor_reduce(small[:, 1, :], ie(2), X, ALU.add))
                step(v.reciprocal(small[:, 2, :], small[:, 1, :]))
                step(v.tensor_tensor(red[:, 4], small[:, 3:5, :], small[:, 2, :].unsqueeze(1).to_broadcast([P, K, NB]), ALU.mult))

            def weigh(b):
                mine = slice(b * NB, (b + 1) * NB)
                step(v.tensor_tensor(small[:, 6, :], red[:, 4, 0], red[:, 4, 1], ALU.add))
                step(v.tensor_scalar(small[:, 6, :], small[:, 6, :], 1e-9, None, ALU.add))
                step(v.reciprocal(small[:, 7, :], small[:, 6, :]))
                step(v.tensor_tensor(w_top[:, :, mine], red[:, 4], small[:, 7, :].unsqueeze(1).to_broadcast([P, K, NB]), ALU.mult))
                step(v.tensor_tensor(w_top[:, :, mine], w_top[:, :, mine], red[:, 5], ALU.mult))

            for c in range(DC):
                dve.wait_ge(f_done, 4 * c + 1)
                v.tensor_scalar(fT[:, c, 0:1], fT[:, c, 0:1], 1.0, None, ALU.add).then_inc(tap_done, 1)
            keep_x1(0, x1b)
            dve.wait_ge(in_const, 80)
            step(v.tensor_copy(xrow[:, :, D], c_rows[:, KEI + 2 * E:]))
            step(v.tensor_scalar(gs[:, :, :], c_gate[:, :, :], WSCALE, None, ALU.mult))
            step(v.tensor_copy(gate16[:, :, 0], gs[:, :, :]))
            v.tensor_tensor(gate16[:, :, 1], gs[:, :, :], gate16[:, :, 0], ALU.subtract).then_inc(gate_split, 1)
            keep_x1(1, x1f)
            dve.wait_ge(fhat_done, 2 + N1)
            with dve.Fori(0, N1 // 2) as k2:
                for s in range(2):
                    multiply(0, 2 * k2 + s, s)
            turn_back(0)
            keep_x1(2, x1b)
            moments(0)
            for k in range(14):
                multiply(1, k, k % 2)
                if k == 0:
                    scores(0)
                elif k in (2, 4):
                    pick(0, k // 2 - 1)
                elif k == 6:
                    count_up(0)
                elif k == 9:
                    place(0)
                elif k == 11:
                    probabilities()
                elif k == 13:
                    weigh(0)
            with dve.Fori(7, N1 // 2) as k2:
                for s in range(2):
                    multiply(1, 2 * k2 + s, s)
            turn_back(1)
            moments(1)
            scores(1)
            for k in range(K):
                pick(1, k)
            count_up(1)
            place(1)
            probabilities()
            weigh(1)
            dve.wait_ge(zero_stored, 16 * K * ZEROS)
            dve.sem_inc(gate_done, 1)
            def turn_lo(n, s, j):
                w = 2 if 2 * j + 1 < RT else 1
                dve.wait_ge(xth_done, XT_PER * n + j + 1)
                cols = lambda t: t[:, :, 2 * j * P:(2 * j + w) * P].rearrange("p c (t r) -> p t c r", t=w)
                v.tensor_tensor(cols(xtl[s]), ps[:, 4 + j % 2, 0:w * D].rearrange("p (t c r) -> p t c r", t=w, c=DC),
                                cols(xth[s]), ALU.subtract).then_inc(xtl_done, 1)

            def read_ids(n, s):
                dve.wait_ge(xth_done, XT_PER * (n + 1))
                if not (isinstance(n, int) and n < 2):
                    dve.wait_ge(tok_done, n - 1)
                v.tensor_copy(tok[s][:, :], xg[s][:, :, D]).then_inc(ids_read, 1)

            def keep_ids(n, s):
                dve.wait_ge(ids_read, n + 1)
                dve.wait_ge(y_room, n + 1)
                v.tensor_copy(tok_y[s][:, :], tok[s][:, :]).then_inc(tok_done, 1)

            def weights_lo(e, parity, j):
                s = (3 * parity + j) % 2
                dve.wait_ge(wh_done, 3 * e + j + 1)
                part = lambda t: t[:, bass.ds(e, 1), j * WPART:(j + 1) * WPART].rearrange("p a c -> p (a c)")
                v.scalar_tensor_tensor(part(wl), wst[s][:, :], WSCALE, part(wh), ALU.mult, ALU.subtract).then_inc(wl_done, 1)

            def a_lo(n, s, j):
                dve.wait_ge(ah_done, Q_PER * n + j + 1)
                r = slice((j % 2) * HALF, (j % 2 + 1) * HALF)
                v.tensor_tensor(al[s][:, j // 2, r], a32[j % 2][:, :], ah[s][:, j // 2, r], ALU.subtract).then_inc(al_done, 1)

            def expert(n, s, split=False, turn=True, last_rows=True):
                if last_rows:
                    keep_ids(n - 1, 1 - s)
                for j in range(Q_PER):
                    dve.wait_ge(s_done, Q_PER * n + j + 1)
                    dve.wait_ge(al_done, Q_PER * n + j + 1)
                    v.scalar_tensor_tensor(a32[j % 2][:, :], ps[:, 2 * (j % 2) + 1, 0:HALF], 1.0 / WSCALE, s32[j % 2][:, :],
                                           ALU.mult, ALU.mult).then_inc(a_done, 1)
                    if j:
                        a_lo(n, s, j - 1)
                    if turn and j in TURNS_AT:
                        for t in TURNS_AT[j]:
                            turn_lo(n + 1, 1 - s, t)
                        if j == max(TURNS_AT):
                            read_ids(n + 1, 1 - s)
                    if split and j in (3, 5, 7):
                        weights_lo(n + 1, 1 - s, (j - 3) // 2)
                a_lo(n, s, Q_PER - 1)

            def add_four(half, s):
                dve.wait_ge(in_yg[s], 16 * (half + 1))
                for j in range(YS):
                    i = YS * (2 * half + s) + j
                    col = xn[:, bass.ds(i, 1), :].rearrange("p a c -> p (a c)")
                    v.scalar_tensor_tensor(col, yg[s][:, j, :], w_top[:, 0, bass.ds(i, 1)], col, ALU.mult, ALU.add).then_inc(yg_used, 1)

            for j in range(3):
                weights_lo(0, 0, j)
            for j in range(XT_PER):
                turn_lo(0, 0, j)
            read_ids(0, 0)
            expert(0, 0, split=True, last_rows=False)
            with dve.Fori(0, (E - 2) // 2) as e2:
                n = 2 * e2 + 1
                expert(n, 1, split=True)
                expert(n + 1, 0, split=True)
            expert(E - 1, 1)
            expert(E, 0)
            with dve.Fori(0, (E - 2) // 2) as e2:
                n = 2 * e2 + E + 1
                expert(n, 1)
                add_four(e2, 0)
                expert(n + 1, 0)
                add_four(e2, 1)
            expert(2 * E - 1, 1, turn=False)
            keep_ids(2 * E - 1, 1)
            add_four(NI // YS // 2 - 1, 0)
            add_four(NI // YS // 2 - 1, 1)
            dve.wait_ge(yg_used, 2 * YS + NI)
            sums = stepped = 0

            def sum_up(lo, hi):
                for i in range(lo, hi):
                    if i not in POOL_COLUMNS:
                        dve.wait_ge(in_y2[i // YS], 16)
                        v.scalar_tensor_tensor(y2[:, i, :], y2[:, i, :], w_top[:, 1, i:i + 1], xn[:, i, :], ALU.mult, ALU.add).then_inc(dve_sums, 1)

            def measure(i):
                v.bn_stats(stats[:, i, :], y2[:, i, :]).then_inc(fin_step, 1)

            sum_up(*GROUPS[0])
            for g, (lo, hi) in enumerate(GROUPS):
                for i in range(lo, hi):
                    if i not in POOL_COLUMNS:
                        sums += 1
                        dve.wait_ge(dve_sums, sums)
                        measure(i)
                if g + 1 < len(GROUPS):
                    sum_up(*GROUPS[g + 1])
                for i in range(lo, hi):
                    if i in POOL_COLUMNS:
                        dve.wait_ge(pool_sums, POOL_COLUMNS.index(i) + 1)
                        measure(i)
                stepped += hi - lo
                dve.wait_ge(fin_step, stepped)
                for n, step_ in enumerate(norm_steps(stats[:, lo:hi, :], lo, hi)):
                    if n == 5:
                        step_().then_inc(fin_var, 1)
                        dve.wait_ge(fin_var, g + 1)
                    else:
                        step_().then_inc(fin_step, 1)
                        stepped += 1
                        dve.wait_ge(fin_step, stepped)
                dve.wait_ge(fin_sq, g + 1)
                v.reciprocal(lnt[:, 6, lo:hi], lnt[:, 5, lo:hi]).then_inc(fin_step, 1)
                stepped += 1
                dve.wait_ge(fin_step, stepped)
                v.scalar_tensor_tensor(lnt[:, 7, lo:hi], lnt[:, 4, lo:hi], -1.0, lnt[:, 6, lo:hi], ALU.mult, ALU.mult).then_inc(fin_scale, 1)


def kernel(L0_attn_x, L0_attn_W1, L0_attn_b1, L0_attn_W2, L0_attn_b2, L0_ffn_gate_w, L0_ffn_gate_proj_w,
           L0_ffn_up_proj_w, L0_ffn_down_proj_w):
    import concourse.bacc as bacc
    from concourse.bass_utils import run_bass_kernel_spmd

    x = np.asarray(L0_attn_x)
    turned = [np.asarray(w).reshape(E, H, DC, P).transpose(0, 3, 2, 1).reshape(E, P, DC * H)
              for w in (L0_ffn_gate_proj_w, L0_ffn_up_proj_w)]
    down = np.asarray(L0_ffn_down_proj_w).reshape(E, D, HC, P).transpose(0, 3, 2, 1).reshape(E, P, HC * D)
    arrays = {
        "xT": x.transpose(0, 2, 1),
        "W1": np.asarray(L0_attn_W1),
        "b1": np.asarray(L0_attn_b1).reshape(DC, P).T,
        "W2": np.asarray(L0_attn_W2).reshape(DC, P, D).transpose(1, 0, 2),
        "b2": np.asarray(L0_attn_b2).reshape(DC, P).T,
        "gateT": np.asarray(L0_ffn_gate_w).reshape(E, DC, P).transpose(2, 1, 0),
        "experts": np.concatenate(turned + [down], axis=2),
    }
    arrays.update(constants())
    arrays = {k: np.ascontiguousarray(v) for k, v in arrays.items()}
    nc = bacc.Bacc("TRN2", target_bir_lowering=False, num_devices=1)
    aps = {k: nc.dram_tensor(f"in_{k}", v.shape, mybir.dt.from_np(v.dtype), kind="ExternalInput").ap() for k, v in arrays.items()}
    out = nc.dram_tensor("out_y", (T, D), F32, kind="ExternalOutput").ap()
    build(nc, out=out, **aps)
    r = run_bass_kernel_spmd(nc, [{f"in_{k}": v for k, v in arrays.items()}], core_ids=[0])
    return r.results[0]["out_y"].reshape(B, L, D)
```
